# Optimizing a Trainium2 kernel written in Bass

```python
import numpy as np
import jax
import jax.numpy as jnp

def _softmax(x, axis=-1):
    return jax.nn.softmax(x, axis=axis)

def _gelu(x):
    return jax.nn.gelu(x, approximate=True)

def _silu(x):
    return jax.nn.silu(x)

def _sigmoid(x):
    return jax.nn.sigmoid(x)

def _layernorm(x, axis=-1, eps=1e-05):
    m = jnp.mean(x, axis=axis, keepdims=True)
    v = jnp.var(x, axis=axis, keepdims=True)
    return (x - m) / jnp.sqrt(v + eps)

def _scatter_add(tgt, idx, src, axis=0):
    return tgt.at[idx].add(src)

def _segment_sum(src, seg, n):
    return jax.ops.segment_sum(src, seg, n)
kernel_name = 'mk_xattn_ffn_d1_seqx_r4_9dc47b'

def setup_inputs(seed: int=0):
    np.random.seed(seed)
    _w = jnp.asarray

    def _rec_inputs():
        import jax
        import jax.numpy as jnp
        _rk = jax.random.key(seed)
        x = -0.000125 + 0.9999 * jax.random.normal(jax.random.fold_in(_rk, 1), (4, 512, 512), jnp.float32)
        _lenS = 512 - jax.random.randint(jax.random.fold_in(_rk, 7), (4,), 0, max(1, 512 // 4) + 1, jnp.int32)
        _lenS2 = 512 - jax.random.randint(jax.random.fold_in(_rk, 8), (4,), 0, max(1, 512 // 4) + 1, jnp.int32)
        _ctx_2048P = jax.random.normal(jax.random.fold_in(_rk, 11), (4, 16, 512), jnp.float32)
        _ctx_2048c = jax.random.dirichlet(jax.random.fold_in(_rk, 511), 0.3 * jnp.ones((16,), jnp.float32), (4, 512))
        _ctx_2048t = jnp.einsum('bsk,bkd->bsd', _ctx_2048c, _ctx_2048P)
        _ctx_2048t = _ctx_2048t * jax.lax.rsqrt(jnp.mean(jnp.square(_ctx_2048t)) + 1e-12) * 0.953939
        ctx_2048 = -0.000514642 + 1.00011 * (_ctx_2048t + 0.3 * jax.random.normal(jax.random.fold_in(_rk, 611), (4, 512, 512), jnp.float32))
        _validS = jnp.arange(512)[None, :] < _lenS[:, None]
        _validS2 = jnp.arange(512)[None, :] < _lenS2[:, None]
        _causal = jnp.tril(jnp.ones((512, 512), dtype=bool))
        mask_BxS2_bk0 = jnp.logical_not(jnp.broadcast_to(_validS2[:, :], (4, 512)))
        return (x, ctx_2048, mask_BxS2_bk0)
    x, ctx_2048, mask_BxS2_bk0 = _rec_inputs()

    def _L0_xattn_setup():
        import jax, jax.numpy as jnp
        import numpy as np
        key = jax.random.key(seed)
        k1, k2, k3 = jax.random.split(key, 3)
        B, S, D, M = (8, 512, 512, 128)
        hidden_states = jax.random.normal(k1, (B, S, D), dtype=jnp.float32)
        memory_tokens = jax.random.normal(k2, (B, M, D), dtype=jnp.float32)
        memory_mask = jax.random.randint(k3, (B, M), 0, 2).astype(jnp.bool_)
        return {'hidden_states': hidden_states, 'memory_tokens': memory_tokens, 'memory_mask': memory_mask}
    _L0_xattn_all = _L0_xattn_setup()
    _L0_xattn_in = {k: v for k, v in _L0_xattn_all.items() if k in ()}
    del _L0_xattn_all

    def _L0_ffn_setup():
        import jax, jax.numpy as jnp
        import numpy as np
        NUM_EXPERTS = 8
        TOP_K = 2
        key = jax.random.key(seed)
        ks = jax.random.split(key, 5)
        B, L, D, H = (2, 512, 512, 1024)
        return {'layer_input': jax.random.normal(ks[0], (B, L, D), jnp.float32), 'router_weight': jax.random.normal(ks[1], (NUM_EXPERTS, D), jnp.float32) * 0.02, 'w_in': jax.random.normal(ks[2], (NUM_EXPERTS, 2 * H, D), jnp.float32) * 0.02, 'w_out': jax.random.normal(ks[3], (NUM_EXPERTS, D, H), jnp.float32) * 0.02, 'bias': jax.random.normal(ks[4], (D,), jnp.float32) * 0.02}
    _L0_ffn_all = _L0_ffn_setup()
    _L0_ffn_in = {k: v for k, v in _L0_ffn_all.items() if k in ('router_weight', 'w_in', 'w_out', 'bias')}
    del _L0_ffn_all
    return {'x': x, 'ctx_2048': ctx_2048, 'mask_BxS2_bk0': mask_BxS2_bk0, 'L0_ffn_router_weight': _L0_ffn_in['router_weight'], 'L0_ffn_w_in': _L0_ffn_in['w_in'], 'L0_ffn_w_out': _L0_ffn_in['w_out'], 'L0_ffn_bias': _L0_ffn_in['bias']}

def reference(x, ctx_2048, mask_BxS2_bk0, L0_ffn_router_weight, L0_ffn_w_in, L0_ffn_w_out, L0_ffn_bias):
    import jax
    import jax.numpy as jnp

    def _L0_xattn_ref(hidden_states, memory_tokens, memory_mask):
        import jax, jax.numpy as jnp
        import numpy as np
        B, S, D = hidden_states.shape
        scale = 1.0 / jnp.sqrt(jnp.asarray(D, hidden_states.dtype))
        scores = jnp.einsum('bsd,bmd->bsm', hidden_states, memory_tokens) * scale
        neg_inf = jnp.asarray(-1e+30, scores.dtype)
        scores = jnp.where(memory_mask[:, None, :], scores, neg_inf)
        attn = jax.nn.softmax(scores, axis=-1)
        readout = jnp.einsum('bsm,bmd->bsd', attn, memory_tokens)
        valid_b = jnp.any(memory_mask, axis=-1)
        out = jnp.where(valid_b[:, None, None], readout, jnp.zeros_like(readout))
        return out

    def _L0_ffn_ref(layer_input, router_weight, w_in, w_out, bias):
        import jax, jax.numpy as jnp
        import numpy as np
        NUM_EXPERTS = 8
        TOP_K = 2
        B, L, D = layer_input.shape
        x = layer_input.reshape(-1, D)
        T = x.shape[0]
        logits = (x @ router_weight.T).astype(jnp.float32)
        top_vals, top_idx = jax.lax.top_k(logits, TOP_K)
        top_gates = jax.nn.softmax(top_vals, axis=1).astype(x.dtype)
        dense_gates = jnp.zeros((T, NUM_EXPERTS), x.dtype)
        dense_gates = dense_gates.at[jnp.arange(T)[:, None], top_idx].set(top_gates)

        def expert_step(acc, ew):
            wi, wo, g = ew
            h = x @ wi.T
            a, b = jnp.split(h, 2, axis=-1)
            o = jax.nn.silu(a) * b @ wo.T
            return (acc + g[:, None] * o, None)
        acc, _ = jax.lax.scan(expert_step, jnp.zeros_like(x), (w_in, w_out, dense_gates.T))
        return acc.reshape(B, L, D) + bias
    x = x + _L0_xattn_ref(_layernorm(x, axis=-1), ctx_2048, mask_BxS2_bk0)
    x = x + _L0_ffn_ref(_layernorm(x, axis=-1), L0_ffn_router_weight, L0_ffn_w_in, L0_ffn_w_out, L0_ffn_bias)
    return x

_drawn_inputs = setup_inputs


def setup_inputs(seed=0):
    import zlib

    import numpy as np

    out = dict(_drawn_inputs(seed))
    spreads = {}
    factors = {'L0_ffn_bias': 3.397}
    for name, (base, spread) in spreads.items():
        noise = np.random.default_rng([zlib.crc32(name.encode()), seed]).standard_normal(out[name].shape)
        drawn = base * np.exp(spread * noise) if base else spread * noise
        out[name] = jnp.asarray(drawn.astype(out[name].dtype))
    for name, factor in factors.items():
        out[name] = (out[name] * factor).astype(out[name].dtype)
    return out
```

```python
from contextlib import ExitStack

import concourse.bass as bass
from concourse import mybir

P = 128
F32 = mybir.dt.float32
F32R = mybir.dt.float32r
F16 = mybir.dt.float16
I32 = mybir.dt.int32
ALU = mybir.AluOpType
ACT = mybir.ActivationFunctionType
AX = mybir.AxisListType.X

TOP_K = 2
HI, LO = 0, 1
PASSES = ((HI, HI), (HI, LO), (LO, HI))
CHUNKS = 4
LN_EPS = 1e-5
NEG = -1e30
LOWEST = -3.0e38


def xattn_moe_kernel(nc, x, ctx_rows, ctx_cols, mask, router_cols, w_in, w_out, bias, out):
    T, D = x.shape
    B, M, _ = ctx_rows.shape
    E = router_cols.shape[1]
    KD = D // P
    KM = M // P
    TT = T // P
    TB = TT // B
    WI = w_in.shape[3]
    WO = w_out.shape[3]
    CF = WI // KD
    CG = CF // 2
    KS = CG // P
    SLOT_TILES = (TOP_K * T - E) // P + E
    ST1 = SLOT_TILES + 1
    SCALE = float(D) ** -0.5
    assert T % P == 0 and D == 512 and M == 512 and KS == 2 and TB == 4 and WO == KS * D

    xn_dram = nc.dram_tensor("xn_rows", (T, D), F32, kind="Internal").ap()
    y_dram = nc.dram_tensor("y_rows", (SLOT_TILES * P, D), F32, kind="Internal").ap()

    with ExitStack() as ctx:
        def sb(name, shape, dt=F32):
            return ctx.enter_context(nc.sbuf_tensor(name, shape, dt))

        def sem(name):
            return ctx.enter_context(nc.semaphore(name))

        def sems(name, n):
            return [sem(f"{name}{i}") for i in range(n)]

        resid = sb("resid", [P, TT, D])
        win = sb("win", [P, 2, CHUNKS, WI], F32R)
        wout = sb("wout", [P, 2, CHUNKS, WO], F32R)
        raw_in = sb("raw_in", [P, CHUNKS, WI])
        raw_out = sb("raw_out", [P, CHUNKS, WO])
        rows = sb("rows", [P, 2, D])
        rowsT = [sb(f"rowsT{i}", [P, 2, KD, P], F32R) for i in range(2)]
        work = sb("work", [P, 2, D])
        probs = sb("probs", [P, 2, D])
        gT = [sb(f"gT{i}", [P, 2, KS, P], F32R) for i in range(2)]
        ident = sb("ident", [P, P])
        ones = sb("ones", [P, P])
        earlier = sb("earlier", [P, P])
        router = sb("router", [P, KD, E])
        mv1 = sb("mv1", [P, TT, 2])
        mv2 = sb("mv2", [P, TB, 2])
        mv = sb("mv", [P, 2])
        bn = sb("bn", [P, 2, 6])
        ve = sb("ve", [P, 4, TT])
        rstd1 = sb("rstd1", [P, TT])
        rstd2 = sb("rstd2", [P, TB])
        smax = sb("smax", [P, 2, 6])
        valid = sb("valid", [P, 1])
        gates = sb("gates", [P, TOP_K, TT])
        slot_of = sb("slot_of", [P, TOP_K, TT], I32)
        token_of = sb("token_of", [P, ST1], I32)
        idx = sb("idx", [P, 2 * TOP_K * 2], I32)
        plan = sb("plan", [1, 3, ST1], I32)
        nxt = sb("nxt", [1, ST1], I32)
        sink_act, sink_dve, sink_pool = (sb(f"sink_{e}", [P, 2 * CHUNKS]) for e in ("act", "dve", "pool"))
        gate_in, gate_out = sb("gate_in", [P, TT]), sb("gate_out", [P, TT])
        ranks, starts, lanes, tiles = (sb(n, [P, TOP_K, TT]) for n in ("ranks", "starts", "lanes", "tiles"))
        ranks_i, lanes_i, tiles_i = (sb(n, [P, TOP_K, TT], I32) for n in ("ranks_i", "lanes_i", "tiles_i"))
        n_tiles = sb("n_tiles", [P, E])
        lane_ids = sb("lane_ids", [P, P])
        falling = sb("falling", [P, E])
        tile_starts = sb("tile_starts", [P, TT])
        token_ids = sb("token_ids", [P, TT])

        win_flat = win[:].rearrange("p h c w -> p (h c w)")
        wout_flat = wout[:].rearrange("p h c w -> p (h c w)")
        CTXW = 2 * 2 * KD * M

        def ctx_part(par, kind, part, k):
            off = kind * 2 * KD * M + part * KD * M + k * M
            return win_flat[:, bass.ds(par * CTXW + off, M)]

        probsT = [wout_flat[:, i * 2 * M:(i + 1) * 2 * M].rearrange("p (h k q) -> p h k q", h=2, k=KM)
                  for i in range(2)]
        silus = [work[:, 0, i * CG:(i + 1) * CG] for i in range(2)]
        gated = [work[:, 1, i * CG:(i + 1) * CG] for i in range(2)]
        lane_hot = raw_in[:, 3, :].bitcast(F16).rearrange("p (q l) -> p q l", l=P)
        tile_hot = raw_in[:, 2, 0:TOP_K * TT * ST1 // 2].bitcast(F16).rearrange("p (q l) -> p q l", l=ST1)
        small_plan = rows[:, 1, P:P + E * ST1]
        plan_f = probs[0:1, 1, 0:5 * ST1].rearrange("p (i t) -> p i t", i=5)
        ctx_raw = [raw_in[:, 2, :].rearrange("p (k m) -> p k m", k=KD),
                   raw_in[:, 3, :].rearrange("p (k m) -> p k m", k=KD)]
        rows2 = raw_out[:, 0, :].rearrange("p (j d) -> p j d", j=2)
        rows2T = raw_out[:, 1, :].rearrange("p (j k q) -> p j k q", j=2, k=KD)
        mask_i = raw_out[:, 2, 0:M].bitcast(I32)
        mask_scale = raw_out[:, 2, M:2 * M]
        mask_neg = raw_out[:, 3, 0:M]
        bias_bc = raw_out[:, 3, M:2 * M]

        bank = [ctx.enter_context(nc.psum_tensor(f"bank{i}", [P, 512], F32)) for i in range(8)]
        b_rowsT = bank[0:2]
        b_scores = bank[2:4]
        b_probsT, b_rows2T, b_read, b_logits = bank[4:8]
        b_h = bank[0:4]
        b_gT = bank[4:6]
        b_xT, b_y = bank[6:8]

        x_in, ctx_in, mask_in, small_in, bias_in = (sem(n) for n in ("x_in", "ctx_in", "mask_in", "small_in", "bias_in"))
        consts = sem("consts")
        stats, rs_in, rs_sqrt, rs_step, rstd_ready = (sem(n) for n in ("stats", "rs_in", "rs_sqrt", "rs_step", "rstd_ready"))
        rows_ready, rowsT_done, rowsT_hi, rowsT_lo = (sem(n) for n in ("rows_ready", "rowsT_done", "rowsT_hi", "rowsT_lo"))
        ctx_hi, ctx_ready = sem("ctx_hi"), sem("ctx_ready")
        mask_done = sem("mask_done")
        scores_done, masked, maxed, negmax, exp_done = (sem(n) for n in ("scores_done", "masked", "maxed", "negmax", "exp_done"))
        probsT_done, probsT_hi, probsT_lo, read_done = (sem(n) for n in ("probsT_done", "probsT_hi", "probsT_lo", "read_done"))
        norm_step, resid_done, mv2_done = sem("norm_step"), sem("resid_done"), sem("mv2_done")
        xn_stored = sems("xn_stored", 2)
        rows2_ready, rows2T_done, rows2T_copied, logits_done, biased = (
            sem(n) for n in ("rows2_ready", "rows2T_done", "rows2T_copied", "logits_done", "biased"))
        route, gate_exp, counts_done, onehots, token_sum, plan_ready = (
            sem(n) for n in ("route", "gate_exp", "counts_done", "onehots", "token_sum", "plan_ready"))
        raw_sem = sems("raw", CHUNKS)
        win_hi, win_ready, wout_hi, wout_ready = (sems(n, CHUNKS) for n in ("win_hi", "win_ready", "wout_hi", "wout_ready"))
        idx_ready, gathered, xT_done, xT_hi, xT_ready = (sem(n) for n in ("idx_ready", "gathered", "xT_done", "xT_hi", "xT_ready"))
        h_ready, silu_done, g_done, gT_done, gT_hi, gT_ready = (
            sem(n) for n in ("h_ready", "silu_done", "g_done", "gT_done", "gT_hi", "gT_ready"))
        y_part, y_copied, y_stored = sem("y_part"), sem("y_copied"), sem("y_stored")
        pair_idx, pair_in, pair_sum, out_stored = sem("pair_idx"), sems("pair_in", 4), sem("pair_sum"), sem("out_stored")
        order = sem("order")

        x_tiles = x.rearrange("(n p) d -> p n d", p=P)
        out_tiles = out.rearrange("(n p) d -> p n d", p=P)
        xn_tiles = xn_dram.rearrange("(n p) d -> p n d", p=P)
        y_tiles = y_dram.rearrange("(n p) d -> p n d", p=P)

        def at(tensor, i):
            return tensor[:, bass.ds(i, 1), :].rearrange("p o d -> p (o d)")

        def col(tensor, i):
            return tensor[:, bass.ds(i, 1)]

        block = ctx.enter_context(nc.Block())

        @block.sync
        def _(sp):
            def load_ctx(b):
                sp.dma_start(ctx_raw[0], ctx_cols[bass.ds(b, 1), :, :].rearrange("o (k p) m -> p (o k) m", p=P)).then_inc(ctx_in, 16)
                sp.dma_start(ctx_raw[1], ctx_rows[bass.ds(b, 1), :, :].rearrange("o (k p) d -> p (o k) d", p=P)).then_inc(ctx_in, 16)

            def load_mask(b):
                sp.dma_start(mask_i, mask[bass.ds(b, 1), :].to_broadcast((P, M))).then_inc(mask_in, 16)

            def load_win(c, e, **kw):
                sp.dma_start(raw_in[:, c, :], w_in[bass.ds(e, 1), c, :, :].rearrange("o p w -> (o p) w"), **kw).then_inc(raw_sem[c], 16)

            def load_wout(c, e, **kw):
                sp.dma_start(raw_out[:, c, :], w_out[bass.ds(e, 1), c, :, :].rearrange("o p w -> (o p) w"), **kw).then_inc(raw_sem[c], 16)

            def store_rows2(b):
                for j in range(TB):
                    n = TB * b + j
                    sp.wait_ge(rows2_ready, n + 1)
                    sp.dma_start(at(xn_tiles, n), rows2[:, j % 2, :]).then_inc(xn_stored[j % 2], 16)

            for p in range(2):
                sp.sem_inc(xn_stored[p], 16)
            sp.dma_start(resid[:, 0:TB, :], x_tiles[:, 0:TB, :]).then_inc(x_in, 16)
            load_ctx(0)
            load_mask(0)
            sp.dma_start(router[:], router_cols.rearrange("(k p) e -> p k e", p=P)).then_inc(small_in, 16)
            sp.dma_start(resid[:, TB:TT, :], x_tiles[:, TB:TT, :]).then_inc(small_in, 16)
            sp.dma_start(bias_bc, bias.to_broadcast((P, D))).then_inc(bias_in, 16)
            for c in (0, 1):
                load_win(c, 0)

            def batch(b, first=False, last=False):
                if not last:
                    sp.wait_ge(ctx_ready, 8 * b + 8)
                    load_ctx(b + 1)
                    sp.wait_ge(mask_done, 3 * b + 3)
                    load_mask(b + 1)
                if not first:
                    store_rows2(b - 1)

            batch(0, first=True)
            with sp.Fori(1, B - 1) as b:
                batch(b)
            batch(B - 1, last=True)
            store_rows2(B - 1)

            sp.wait_ge(biased, TT)
            sp.wait_ge(logits_done, TT + 2)
            for p in range(2):
                sp.wait_ge(xn_stored[p], 16 * (TT // 2) + 16)
            sp.wait_ge(masked, TT + 2)
            sp.wait_ge(maxed, TT + 1)
            for c in range(CHUNKS):
                load_wout(c, 0)
            sp.wait_ge(token_sum, 1)
            load_win(2, 0)
            load_win(3, 0)
            sp.wait_ge(plan_ready, 1)
            first = sp.snap(sp.value_load(plan[0:1, 0, 0:1], min_val=0, max_val=E - 1))
            for c in range(CHUNKS):
                sp.wait_ge(raw_sem[c], 32)
                load_win(c, first, cond=(first != 0))
                load_wout(c, first, cond=(first != 0))
            with sp.Fori(0, SLOT_TILES) as t:
                wanted = sp.snap(sp.value_load(plan[0:1, 2, bass.ds(t, 1)], min_val=0, max_val=1))
                e = sp.snap(sp.value_load(nxt[0:1, bass.ds(t, 1)], min_val=0, max_val=E - 1))
                for c in range(CHUNKS):
                    sp.wait_ge(wout_ready[c], t + 1)
                    sp.wait_ge(win_ready[c], t + 1)
                    sp.sem_inc(order, 1)
                    load_win(c, e, cond=(wanted != 0))
                    load_wout(c, e, cond=(wanted != 0))
            with sp.Fori(0, TT) as i:
                sp.wait_ge(pair_sum, 2 * i + 10)
                sp.sem_inc(order, 1)
                sp.dma_start(at(out_tiles, i), at(resid, i)).then_inc(out_stored, 16)
            sp.wait_ge(out_stored, 16 * TT)
            for c in range(CHUNKS):
                sp.wait_ge(raw_sem[c], 32 * (SLOT_TILES + 2))

        @block.gpsimd
        def _(pool):
            pool.memset(ones[:], 1.0).then_inc(consts, 1)
            pool.wait_ge(consts, 1)
            pool.affine_select(ident[:], ones[:], pattern=[[-1, P]], compare_op=ALU.is_equal, fill=0.0,
                               base=0, channel_multiplier=1).then_inc(consts, 1)
            pool.affine_select(earlier[:], ones[:], pattern=[[1, P]], compare_op=ALU.is_gt, fill=0.0,
                               base=0, channel_multiplier=-1).then_inc(consts, 1)
            pool.iota(lane_ids[:], pattern=[[1, P]], base=0, channel_multiplier=0,
                      allow_small_or_imprecise_dtypes=True).then_inc(consts, 1)
            pool.iota(falling[:], pattern=[[-1, E]], base=E, channel_multiplier=0,
                      allow_small_or_imprecise_dtypes=True).then_inc(consts, 1)
            pool.iota(tile_starts[:], pattern=[[P, TT]], base=0, channel_multiplier=0,
                      allow_small_or_imprecise_dtypes=True).then_inc(consts, 1)
            pool.iota(token_ids[:], pattern=[[P, TT]], base=0, channel_multiplier=1,
                      allow_small_or_imprecise_dtypes=True).then_inc(consts, 1)
            pool.wait_ge(bias_in, 16)
            with pool.Fori(0, TT) as n:
                pool.wait_ge(rows2_ready, n + 1)
                pool.tensor_tensor(at(resid, n), at(resid, n), bias_bc, ALU.add).then_inc(biased, 1)

            def gather(t):
                pool.wait_ge(idx_ready, t + 1)
                pool.sem_inc(order, 1)
                pool.indirect_dma_start(rows[:, 0, :], None, xn_dram,
                                        bass.IndirectOffsetOnAxis(idx[:, 0:1], 0)).then_inc(gathered, 16)

            def wout_lo(c, t, flag=None):
                def op():
                    return pool.tensor_tensor(wout[:, LO, c, :], raw_out[:, c, :], wout[:, HI, c, :], ALU.subtract)
                if flag is None:
                    pool.wait_ge(wout_hi[c], t + 1)
                    op().then_inc(wout_ready[c], 1)
                    return
                with pool.If(flag != 0):
                    pool.wait_ge(wout_hi[c], t + 1)
                    op().then_inc(wout_ready[c], 1)
                with pool.Else():
                    pool.wait_ge(wout_hi[c], t + 1)
                    pool.wait_ge(wout_ready[c], t)
                    pool.sem_inc(order, 1)
                    pool.tensor_copy(sink_pool[:, c:c + 1], ones[:, 0:1]).then_inc(wout_ready[c], 1)

            pool.wait_ge(plan_ready, 1)
            for p in range(2):
                pool.wait_ge(xn_stored[p], 16 * (TT // 2) + 16)
            pool.tensor_copy(idx[:, 0:1], token_of[:, 0:1]).then_inc(idx_ready, 1)
            gather(0)
            for c in range(CHUNKS - 1):
                wout_lo(c, 0)

            def tile(t, last=False):
                this_new = pool.snap(pool.value_load(plan[0:1, 1, bass.ds(t, 1)], min_val=0, max_val=1))
                if not last:
                    next_new = pool.snap(pool.value_load(plan[0:1, 1, bass.ds(t + 1, 1)], min_val=0, max_val=1))
                    pool.wait_ge(gathered, 16 * t + 16)
                    pool.tensor_copy(idx[:, 0:1], col(token_of, t + 1)).then_inc(idx_ready, 1)
                    pool.wait_ge(xT_done, t + 1)
                    gather(t + 1)
                wout_lo(CHUNKS - 1, t, this_new)
                if not last:
                    for c in range(CHUNKS - 1):
                        wout_lo(c, t + 1, next_new)

            with pool.Fori(0, SLOT_TILES - 1) as t:
                tile(t)
            tile(SLOT_TILES - 1, last=True)

            pool.wait_ge(y_stored, 16 * SLOT_TILES + 16)
            for c in range(CHUNKS):
                pool.wait_ge(raw_sem[c], 32 * (SLOT_TILES + 2))
            with pool.Fori(0, TT // 4) as q:
                for s in range(4):
                    pool.wait_ge(pair_sum, 8 * q + 2 * s + 2)
                    for c in range(TOP_K):
                        pool.tensor_copy(idx[:, 2 * s + c:2 * s + c + 1],
                                         slot_of[:, c, bass.ds(4 * q + s, 1)]).then_inc(pair_idx, 1)
                    pool.wait_ge(pair_idx, 8 * q + 2 * s + 2)
                    pool.sem_inc(order, 1)
                    for c in range(TOP_K):
                        pool.indirect_dma_start(raw_in[:, s, c * D:(c + 1) * D], None, y_dram,
                                                bass.IndirectOffsetOnAxis(idx[:, 2 * s + c:2 * s + c + 1], 0)).then_inc(pair_in[s], 16)

        @block.tensor
        def _(pe):
            pe.sem_inc(rowsT_done, 2)
            pe.sem_inc(scores_done, 2)
            pe.sem_inc(probsT_done, 2)
            pe.sem_inc(read_done, 2)
            pe.sem_inc(rows2T_done, 2)
            pe.sem_inc(logits_done, 2)
            pe.sem_inc(gT_done, 2)
            pe.sem_inc(y_part, 2)
            pe.wait_ge(consts, 3)

            def transposes(dst, src, n):
                for k in range(n):
                    mm = pe.transpose(dst[:, k * P:(k + 1) * P], src[:, k * P:(k + 1) * P], ident[:])
                return mm

            def rows_turn(n, j):
                pe.wait_ge(rows_ready, n + 1)
                pe.wait_ge(rowsT_lo, n + 1)
                transposes(b_rowsT[j % 2], rows[:, j % 2, :], KD).then_inc(rowsT_done, 1)

            def scores(n, b, j):
                par = b % 2
                pe.wait_ge(ctx_ready, 8 * b + 8)
                pe.wait_ge(rowsT_lo, n + 3)
                pe.wait_ge(masked, n + 1)
                m = 0
                for k in range(KD):
                    for s, v in PASSES:
                        mm = pe.matmul(b_scores[j % 2][:], rowsT[j % 2][:, s, k, :], ctx_part(par, 0, v, k),
                                       start=(m == 0), stop=(m == 3 * KD - 1))
                        m += 1
                mm.then_inc(scores_done, 1)

            def probs_turn(n, j):
                pe.wait_ge(exp_done, n + 3)
                pe.wait_ge(probsT_lo, n + 1)
                transposes(b_probsT, probs[:, j % 2, :], KM).then_inc(probsT_done, 1)

            def read(n, b, j):
                par = b % 2
                pe.wait_ge(probsT_lo, n + 2)
                pe.wait_ge(resid_done, n + 2)
                m = 0
                for k in range(KM):
                    for s, v in PASSES:
                        mm = pe.matmul(b_read[:], probsT[j % 2][:, s, k, :], ctx_part(par, 1, v, k),
                                       start=(m == 0), stop=(m == 3 * KM - 1))
                        m += 1
                mm.then_inc(read_done, 1)

            def rows2_turn(n, j):
                pe.wait_ge(rows2_ready, n + 1)
                pe.wait_ge(rows2T_copied, n + 1)
                transposes(b_rows2T, rows2[:, j % 2, :], KD).then_inc(rows2T_done, 1)

            def logits(n, j):
                pe.wait_ge(rows2T_copied, n + 2)
                for k in range(KD):
                    mm = pe.matmul(b_logits[:, bass.ds(n * E, E)], rows2T[:, j % 2, k, :], router[:, k, :],
                                   start=(k == 0), stop=(k == KD - 1))
                mm.then_inc(logits_done, 1)

            def route_rows(b, js):
                for j in js:
                    rows2_turn(TB * b + j, j)
                    logits(TB * b + j, j)

            def batch(b, first=False):
                n = TB * b
                rows_turn(n, 0)
                scores(n, b, 0)
                rows_turn(n + 1, 1)
                scores(n + 1, b, 1)
                if not first:
                    route_rows(b - 1, (0, 1))
                probs_turn(n, 0)
                read(n, b, 0)
                rows_turn(n + 2, 2)
                scores(n + 2, b, 2)
                if not first:
                    route_rows(b - 1, (2, 3))
                probs_turn(n + 1, 1)
                read(n + 1, b, 1)
                rows_turn(n + 3, 3)
                scores(n + 3, b, 3)
                for j in (2, 3):
                    probs_turn(n + j, j)
                    read(n + j, b, j)

            pe.wait_ge(small_in, 32)
            batch(0, first=True)
            with pe.Fori(1, B) as b:
                batch(b)
            route_rows(B - 1, range(TB))

            pe.wait_ge(counts_done, 1)
            pe.matmul(bank[0][:, 0:TT * E], earlier[:], work[:, 0, 0:TT * E], start=True, stop=True)
            pe.matmul(bank[1][:, 0:TT * E], ones[:], work[:, 0, 0:TT * E], start=True, stop=True).then_inc(counts_done, 1)
            pe.wait_ge(onehots, 1)
            for q in range(TOP_K * TT):
                mm = pe.matmul(bank[2][:, 0:ST1], lane_hot[:, q, :], tile_hot[:, q, :],
                               start=(q == 0), stop=(q == TOP_K * TT - 1))
            mm.then_inc(token_sum, 1)

            def x_turn(t):
                pe.wait_ge(gathered, 16 * t + 16)
                pe.wait_ge(xT_ready, t + 1)
                transposes(b_xT, rows[:, 0, :], KD).then_inc(xT_done, 1)

            def up(t, c):
                if c == 0:
                    pe.wait_ge(xT_ready, t + 2)
                pe.wait_ge(win_ready[c], t + 1)
                pe.wait_ge(g_done, 4 * t + c + 1)
                m = 0
                for k in range(KD):
                    for s, v in PASSES:
                        mm = pe.matmul(b_h[c][:], rowsT[0][:, s, k, :], win[:, v, c, k * CF:(k + 1) * CF],
                                       start=(m == 0), stop=(m == 3 * KD - 1))
                        m += 1
                mm.then_inc(h_ready, 1)

            def g_turn(t, c):
                pe.wait_ge(g_done, 4 * t + c + 5)
                pe.wait_ge(gT_ready, 4 * t + c + 1)
                transposes(b_gT[c % 2], gated[c % 2], KS).then_inc(gT_done, 1)

            def down(t, c):
                pe.wait_ge(gT_ready, 4 * t + c + 3)
                pe.wait_ge(wout_ready[c], t + 1)
                if c == 0:
                    pe.wait_ge(y_copied, t + 1)
                m = 0
                for k in range(KS):
                    for s, v in PASSES:
                        mm = pe.matmul(b_y[:], gT[c % 2][:, s, k, :], wout[:, v, c, k * D:(k + 1) * D],
                                       start=(c == 0 and m == 0), stop=(c == CHUNKS - 1 and m == 3 * KS - 1))
                        m += 1
                mm.then_inc(y_part, 1)

            def tile(t, last=False):
                up(t, 1)
                g_turn(t, 0)
                up(t, 2)
                g_turn(t, 1)
                down(t, 0)
                up(t, 3)
                g_turn(t, 2)
                down(t, 1)
                if not last:
                    x_turn(t + 1)
                down(t, 2)
                g_turn(t, 3)
                if not last:
                    up(t + 1, 0)
                down(t, 3)

            x_turn(0)
            up(0, 0)
            with pe.Fori(0, SLOT_TILES - 1) as t:
                tile(t)
            tile(SLOT_TILES - 1, last=True)

        @block.scalar
        def _(act):
            act.sem_inc(exp_done, 2)
            act.sem_inc(rows2T_copied, 1)
            act.sem_inc(y_stored, 16)

            def root(r, n):
                act.wait_ge(rs_in, r + 1)
                act.activation(ve[:, 1, 0:n], ve[:, 0, 0:n], ACT.Sqrt).then_inc(rs_sqrt, 1)

            def split_ctx(b, pieces):
                act.wait_ge(ctx_in, 32 * b + 32)
                for i in pieces:
                    kind, k = i // KD, i % KD
                    act.activation(ctx_part(b % 2, kind, HI, k), ctx_raw[kind][:, k, :], ACT.Copy).then_inc(ctx_hi, 1)

            def split_next(b, pieces, last):
                if not last:
                    act.wait_ge(read_done, TB * b + 2)
                    split_ctx(b + 1, pieces)

            def rows_hi(n, j):
                act.wait_ge(rowsT_done, n + 3)
                act.wait_ge(scores_done, n + 1)
                act.activation(rowsT[j % 2][:, HI, :, :].rearrange("p k q -> p (k q)"), b_rowsT[j % 2][:], ACT.Copy).then_inc(rowsT_hi, 1)

            def exps(n, j):
                act.wait_ge(negmax, n + 1)
                act.wait_ge(probsT_done, n + 1)
                act.activation(probs[:, j % 2, :], work[:, j % 2, :], ACT.Exp, bias=smax[:, j % 2, 1:2],
                               accum_out=smax[:, j % 2, 2:3]).then_inc(exp_done, 1)

            def probs_hi(n, j):
                act.wait_ge(probsT_done, n + 3)
                act.wait_ge(read_done, n + 1)
                act.activation(probsT[j % 2][:, HI, :, :].rearrange("p k q -> p (k q)"), b_probsT[:], ACT.Copy).then_inc(probsT_hi, 1)

            def rows2_copies(b, js):
                for j in js:
                    n = TB * b + j
                    act.wait_ge(rows2T_done, n + 3)
                    act.wait_ge(logits_done, n + 1)
                    act.activation(rows2T[:, j % 2, :, :].rearrange("p k q -> p (k q)"), b_rows2T[:], ACT.Copy).then_inc(rows2T_copied, 1)

            def batch(b, first=False, last=False):
                n = TB * b
                rows_hi(n, 0)
                if not first:
                    root(b + 1, TB)
                rows_hi(n + 1, 1)
                split_next(b, (0, 1), last)
                if not first:
                    rows2_copies(b - 1, (0, 1))
                exps(n, 0)
                if first:
                    root(1, TT - TB)
                probs_hi(n, 0)
                exps(n + 1, 1)
                split_next(b, (2, 3), last)
                rows_hi(n + 2, 2)
                if not first:
                    rows2_copies(b - 1, (2, 3))
                probs_hi(n + 1, 1)
                exps(n + 2, 2)
                split_next(b, (4, 5), last)
                rows_hi(n + 3, 3)
                probs_hi(n + 2, 2)
                exps(n + 3, 3)
                split_next(b, (6, 7), last)
                probs_hi(n + 3, 3)

            root(0, TB)
            split_ctx(0, range(2 * KD))
            batch(0, first=True)
            with act.Fori(1, B - 1) as b:
                batch(b)
            batch(B - 1, last=True)
            root(B + 1, TB)
            rows2_copies(B - 1, range(TB))

            act.wait_ge(gate_exp, 1)
            act.activation(gate_out[:], gate_in[:], ACT.Exp).then_inc(gate_exp, 1)

            def win_split(c, t, flag=None):
                def op():
                    return act.activation(win[:, HI, c, :], raw_in[:, c, :], ACT.Copy)
                if flag is None:
                    act.wait_ge(raw_sem[c], 32 * t + 64)
                    op().then_inc(win_hi[c], 1)
                    return
                with act.If(flag != 0):
                    act.wait_ge(h_ready, 4 * t + c - 3)
                    act.wait_ge(raw_sem[c], 32 * t + 64)
                    op().then_inc(win_hi[c], 1)
                with act.Else():
                    act.wait_ge(win_hi[c], t)
                    act.copy(sink_act[:, c:c + 1], ones[:, 0:1]).then_inc(win_hi[c], 1)

            def wout_split(c, t, flag=None):
                def op():
                    return act.activation(wout[:, HI, c, :], raw_out[:, c, :], ACT.Copy)
                if flag is None:
                    act.wait_ge(raw_sem[c], 32 * t + 64)
                    op().then_inc(wout_hi[c], 1)
                    return
                with act.If(flag != 0):
                    act.wait_ge(y_part, 4 * t + c - 1)
                    act.wait_ge(raw_sem[c], 32 * t + 64)
                    op().then_inc(wout_hi[c], 1)
                with act.Else():
                    act.wait_ge(wout_hi[c], t)
                    act.copy(sink_act[:, 4 + c:5 + c], ones[:, 0:1]).then_inc(wout_hi[c], 1)

            def x_hi(t):
                act.wait_ge(xT_done, t + 1)
                act.activation(rowsT[0][:, HI, :, :].rearrange("p k q -> p (k q)"), b_xT[:], ACT.Copy).then_inc(xT_hi, 1)

            def silu(t, c):
                act.wait_ge(h_ready, 4 * t + c + 1)
                act.wait_ge(g_done, 4 * t + c + 3)
                act.activation(silus[c % 2], b_h[c][:, 0:CG], ACT.Silu).then_inc(silu_done, 1)

            def g_hi(t, c):
                act.wait_ge(gT_done, 4 * t + c + 3)
                act.wait_ge(y_part, 4 * t + c + 1)
                act.activation(gT[c % 2][:, HI, :, :].rearrange("p k q -> p (k q)"), b_gT[c % 2][:, 0:CG], ACT.Copy).then_inc(gT_hi, 1)

            def store(t):
                act.wait_ge(y_copied, t + 2)
                act.sem_inc(order, 1)
                act.dma_start(at(y_tiles, t), probs[:, 0, :]).then_inc(y_stored, 16)

            def tile(t, last=False):
                this_new = act.snap(act.value_load(plan[0:1, 1, bass.ds(t, 1)], min_val=0, max_val=1))
                if not last:
                    next_new = act.snap(act.value_load(plan[0:1, 1, bass.ds(t + 1, 1)], min_val=0, max_val=1))
                wout_split(3, t, this_new)
                silu(t, 1)
                g_hi(t, 0)
                if not last:
                    win_split(0, t + 1, next_new)
                silu(t, 2)
                g_hi(t, 1)
                if not last:
                    win_split(1, t + 1, next_new)
                silu(t, 3)
                g_hi(t, 2)
                if not last:
                    win_split(2, t + 1, next_new)
                    wout_split(0, t + 1, next_new)
                    act.wait_ge(h_ready, 4 * t + 4)
                    x_hi(t + 1)
                g_hi(t, 3)
                if not last:
                    silu(t + 1, 0)
                store(t)
                if not last:
                    win_split(3, t + 1, next_new)
                    wout_split(1, t + 1, next_new)
                    wout_split(2, t + 1, next_new)

            act.wait_ge(plan_ready, 1)
            win_split(0, 0)
            x_hi(0)
            for c in (1, 2, 3):
                win_split(c, 0)
            silu(0, 0)
            for c in range(CHUNKS - 1):
                wout_split(c, 0)
            with act.Fori(0, SLOT_TILES - 1) as t:
                tile(t)
            tile(SLOT_TILES - 1, last=True)

        @block.vector
        def _(dve):
            dve.sem_inc(rowsT_lo, 2)
            dve.sem_inc(masked, 2)
            dve.sem_inc(probsT_lo, 1)
            dve.sem_inc(resid_done, 2)
            dve.sem_inc(mv2_done, 1)
            dve.sem_inc(g_done, 4)
            dve.sem_inc(gT_ready, 2)
            dve.sem_inc(xT_ready, 1)
            dve.sem_inc(y_copied, 1)
            dve.sem_inc(pair_sum, 8)

            def rstd_of(r, var, n, dst):
                dve.tensor_scalar(ve[:, 0, 0:n], var, LN_EPS, None, ALU.add).then_inc(rs_in, 1)
                dve.wait_ge(rs_sqrt, r + 1)
                dve.reciprocal(ve[:, 2, 0:n], ve[:, 1, 0:n]).then_inc(rs_step, 1)
                dve.wait_ge(rs_step, 4 * r + 1)
                dve.tensor_tensor(ve[:, 3, 0:n], ve[:, 2, 0:n], ve[:, 2, 0:n], ALU.mult).then_inc(rs_step, 1)
                dve.wait_ge(rs_step, 4 * r + 2)
                dve.tensor_tensor(ve[:, 3, 0:n], ve[:, 3, 0:n], ve[:, 0, 0:n], ALU.mult).then_inc(rs_step, 1)
                dve.wait_ge(rs_step, 4 * r + 3)
                dve.tensor_scalar(ve[:, 3, 0:n], ve[:, 3, 0:n], -0.5, 1.5, ALU.mult, ALU.add).then_inc(rs_step, 1)
                dve.wait_ge(rs_step, 4 * r + 4)
                dve.tensor_tensor(dst, ve[:, 2, 0:n], ve[:, 3, 0:n], ALU.mult).then_inc(rstd_ready, 1)
                dve.wait_ge(rstd_ready, r + 1)

            def stats1(n):
                dve.bn_stats(bn[:, 1, :], at(resid, n)).then_inc(stats, 1)
                dve.wait_ge(stats, 3 * n + 1)
                dve.sem_inc(order, 1)
                dve.bn_aggr(mv[:], bn[:, 1, :]).then_inc(stats, 1)
                dve.wait_ge(stats, 3 * n + 2)
                dve.tensor_copy(at(mv1, n), mv[:]).then_inc(stats, 1)
                dve.wait_ge(stats, 3 * n + 3)

            def normalise(n, j):
                dve.wait_ge(rowsT_done, n + 1)
                dve.tensor_scalar(rows[:, j % 2, :], at(resid, n), mv1[:, bass.ds(n, 1), 0:1].rearrange("p a b -> p (a b)"),
                                  col(rstd1, n), ALU.subtract, ALU.mult).then_inc(rows_ready, 1)

            def rows_lo(n, j):
                dve.wait_ge(rowsT_hi, n + 1)
                hl = rowsT[j % 2]
                dve.tensor_tensor(hl[:, LO, :, :].rearrange("p k q -> p (k q)"), b_rowsT[j % 2][:],
                                  hl[:, HI, :, :].rearrange("p k q -> p (k q)"), ALU.subtract).then_inc(rowsT_lo, 1)

            def split_ctx(b, pieces):
                for i in pieces:
                    kind, k = i // KD, i % KD
                    dve.wait_ge(ctx_hi, 8 * b + i + 1)
                    dve.tensor_tensor(ctx_part(b % 2, kind, LO, k), ctx_raw[kind][:, k, :],
                                      ctx_part(b % 2, kind, HI, k), ALU.subtract).then_inc(ctx_ready, 1)

            def split_next(b, pieces, last):
                if not last:
                    split_ctx(b + 1, pieces)

            def mask_rows(b):
                dve.wait_ge(mask_in, 16 * b + 16)
                dve.wait_ge(maxed, TB * b + 1)
                dve.wait_ge(norm_step, 3 * TB * b + 1)
                dve.tensor_scalar(mask_scale, mask_i, SCALE, None, ALU.mult).then_inc(mask_done, 1)
                dve.tensor_scalar(mask_neg, mask_i, -1.0, -NEG, ALU.add, ALU.mult).then_inc(mask_done, 1)
                dve.tensor_reduce(valid[:], mask_i, AX, ALU.max).then_inc(mask_done, 1)
                dve.wait_ge(mask_done, 3 * b + 3)

            def mask_max(n, j):
                dve.wait_ge(scores_done, n + 3)
                dve.wait_ge(exp_done, n + 1)
                dve.wait_ge(resid_done, n + 1)
                dve.tensor_tensor(work[:, j % 2, :], b_scores[j % 2][:], mask_scale, ALU.mult).then_inc(masked, 1)
                dve.wait_ge(masked, n + 3)
                dve.sem_inc(order, 1)
                dve.tensor_tensor_reduce(out=work[:, j % 2, :], in0=work[:, j % 2, :], in1=mask_neg, scale=1.0, scalar=LOWEST,
                                         op0=ALU.add, op1=ALU.max, accum_out=smax[:, j % 2, 0:1]).then_inc(maxed, 1)
                dve.wait_ge(maxed, n + 2)
                dve.tensor_scalar(smax[:, j % 2, 1:2], smax[:, j % 2, 0:1], -1.0, None, ALU.mult).then_inc(negmax, 1)

            def probs_lo(n, j):
                dve.wait_ge(probsT_hi, n + 1)
                dve.tensor_tensor(probsT[j % 2][:, LO, :, :].rearrange("p k q -> p (k q)"), b_probsT[:],
                                  probsT[j % 2][:, HI, :, :].rearrange("p k q -> p (k q)"), ALU.subtract).then_inc(probsT_lo, 1)

            def residual(n, j):
                dve.wait_ge(exp_done, n + 3)
                dve.reciprocal(smax[:, j % 2, 3:4], smax[:, j % 2, 2:3]).then_inc(norm_step, 1)
                dve.wait_ge(norm_step, 3 * n + 2)
                dve.tensor_tensor(smax[:, j % 2, 4:5], smax[:, j % 2, 3:4], valid[:], ALU.mult).then_inc(norm_step, 1)
                dve.wait_ge(norm_step, 3 * n + 3)
                dve.wait_ge(read_done, n + 3)
                dve.scalar_tensor_tensor(out=at(resid, n), in0=b_read[:], scalar=smax[:, j % 2, 4:5], in1=at(resid, n),
                                         op0=ALU.mult, op1=ALU.add).then_inc(resid_done, 1)
                dve.wait_ge(resid_done, n + 3)
                dve.wait_ge(mv2_done, n + 1)
                dve.sem_inc(order, 1)
                dve.bn_stats(bn[:, 0, :], at(resid, n)).then_inc(norm_step, 1)
                dve.wait_ge(norm_step, 3 * n + 4)
                dve.sem_inc(order, 1)
                dve.bn_aggr(mv2[:, j, :], bn[:, 0, :]).then_inc(mv2_done, 1)

            def rstd_2(b):
                dve.wait_ge(mv2_done, TB * b + TB + 1)
                rstd_of(b + 2, mv2[:, :, 1:2].rearrange("p a b -> p (a b)"), TB, rstd2[:])

            def normalise2(b, js):
                for j in js:
                    n = TB * b + j
                    dve.wait_ge(rows2T_done, n + 1)
                    dve.wait_ge(xn_stored[j % 2], 32 * b + 16 * (j // 2) + 16)
                    dve.tensor_scalar(rows2[:, j % 2, :], at(resid, n), mv2[:, j, 0:1],
                                      rstd2[:, j:j + 1], ALU.subtract, ALU.mult).then_inc(rows2_ready, 1)

            def batch(b, first=False, last=False):
                n = TB * b
                normalise(n, 0)
                normalise(n + 1, 1)
                rows_lo(n, 0)
                mask_rows(b)
                if not first:
                    rstd_2(b - 1)
                    normalise2(b - 1, (0, 1))
                rows_lo(n + 1, 1)
                mask_max(n, 0)
                if first:
                    with dve.Fori(TB, TT) as m:
                        dve.wait_ge(small_in, 32)
                        stats1(m)
                    rstd_of(1, mv1[:, TB:TT, 1:2].rearrange("p a b -> p (a b)"), TT - TB, rstd1[:, TB:TT])
                split_next(b, (0, 1), last)
                normalise(n + 2, 2)
                mask_max(n + 1, 1)
                probs_lo(n, 0)
                if not first:
                    normalise2(b - 1, (2, 3))
                split_next(b, (2, 3), last)
                rows_lo(n + 2, 2)
                residual(n, 0)
                normalise(n + 3, 3)
                probs_lo(n + 1, 1)
                mask_max(n + 2, 2)
                split_next(b, (4, 5), last)
                rows_lo(n + 3, 3)
                residual(n + 1, 1)
                probs_lo(n + 2, 2)
                mask_max(n + 3, 3)
                split_next(b, (6, 7), last)
                residual(n + 2, 2)
                probs_lo(n + 3, 3)
                residual(n + 3, 3)

            dve.sem_inc(norm_step, 1)
            dve.sem_inc(maxed, 1)
            dve.wait_ge(x_in, 16)
            for n in range(TB):
                stats1(n)
            rstd_of(0, mv1[:, 0:TB, 1:2].rearrange("p a b -> p (a b)"), TB, rstd1[:, 0:TB])
            split_ctx(0, range(2 * KD))
            batch(0, first=True)
            with dve.Fori(1, B - 1) as b:
                batch(b)
            batch(B - 1, last=True)
            rstd_2(B - 1)
            normalise2(B - 1, range(TB))

            steps = [0]

            def step(ins):
                ins.then_inc(route, 1)
                steps[0] += 1
                dve.wait_ge(route, steps[0])

            TE = TT * E
            tab = [work[:, i // 4, (i % 4) * TE:(i % 4 + 1) * TE] for i in range(8)] + \
                  [rows[:, i // 4, (i % 4) * TE:(i % 4 + 1) * TE] for i in range(8)]
            by_te = [a.rearrange("p (t e) -> p t e", e=E) for a in tab]

            def per_t(a):
                return a.unsqueeze(2).to_broadcast((P, TT, E))

            def per_e(a):
                return a.unsqueeze(1).to_broadcast((P, TT, E))

            (both, second_e, L, rank8, top1, top2, t0, t1, cum_a, cum_b, tot, rank) = by_te[:12]
            small = tab[12]
            m1, m2, r1, r2 = (small[:, i * TT:(i + 1) * TT] for i in range(4))
            dve.wait_ge(logits_done, TT + 2)
            dve.wait_ge(consts, 7)
            dve.wait_ge(exp_done, TT + 2)
            step(dve.tensor_copy(tab[2], b_logits[:, 0:TE]))

            def pick(values, top, r, m):
                step(dve.tensor_reduce(m, values, AX, ALU.max))
                step(dve.tensor_tensor(t0, values, per_t(m), ALU.is_equal))
                step(dve.tensor_tensor(t0, t0, per_e(falling[:]), ALU.mult))
                step(dve.tensor_reduce(r, t0, AX, ALU.max))
                step(dve.tensor_tensor(t1, per_e(falling[:]), per_t(r), ALU.is_equal))
                step(dve.tensor_copy(top, t1))

            pick(L, top1, r1, m1)
            step(dve.tensor_scalar(t1, top1, 2.0, -1.0, ALU.mult, ALU.add))
            step(dve.scalar_tensor_tensor(out=L, in0=t1, scalar=LOWEST, in1=L, op0=ALU.mult, op1=ALU.min))
            pick(L, top2, r2, m2)
            dve.tensor_tensor(both, top1, top2, ALU.add).then_inc(counts_done, 1)
            dve.tensor_tensor(gate_in[:], m2, m1, ALU.subtract).then_inc(gate_exp, 1)
            dve.wait_ge(counts_done, 2)
            step(dve.tensor_copy(tot, bank[1][:, 0:TE].rearrange("p (t e) -> p t e", e=E)))
            src, dst = tot, cum_a
            d = 1
            while d < TT:
                step(dve.tensor_copy(dst[:, 0:d, :], src[:, 0:d, :]))
                step(dve.tensor_tensor(dst[:, d:TT, :], src[:, d:TT, :], src[:, 0:TT - d, :], ALU.add))
                src, dst = dst, (cum_b if dst is cum_a else cum_a)
                d *= 2
            cum = src
            n_e = cum[:, TT - 1, :]
            step(dve.tensor_tensor(t0, cum, tot, ALU.subtract))
            step(dve.tensor_tensor(rank, t0, bank[0][:, 0:TE].rearrange("p (t e) -> p t e", e=E), ALU.add))
            over = rank8
            over_et = tab[3].rearrange("p (e t) -> p e t", t=TT)
            step(dve.tensor_tensor(over_et, n_e.unsqueeze(2).to_broadcast((P, E, TT)),
                                   tile_starts[:].unsqueeze(1).to_broadcast((P, E, TT)), ALU.is_gt))
            ends = small[:, 4 * TT:4 * TT + 3 * E].rearrange("p (i e) -> p i e", i=3)
            step(dve.tensor_reduce(ends[:, 0, :], over_et, AX, ALU.add))
            step(dve.tensor_copy(n_tiles[:], ends[:, 0, :]))
            src, dst = 0, 1
            d = 1
            while d < E:
                step(dve.tensor_copy(ends[:, dst, 0:d], ends[:, src, 0:d]))
                step(dve.tensor_tensor(ends[:, dst, d:E], ends[:, src, d:E], ends[:, src, 0:E - d], ALU.add))
                src, dst = dst, 1 - dst
                d *= 2
            end_e = ends[:, src, :]
            step(dve.tensor_tensor(ends[:, 2, :], end_e, n_tiles[:], ALU.subtract))
            start_e = ends[:, 2, :]
            for c, top in enumerate((top1, top2)):
                step(dve.tensor_tensor(t0, top, rank, ALU.mult))
                step(dve.tensor_reduce(ranks[:, c, :], t0, AX, ALU.add))
                step(dve.tensor_tensor(t0, top, per_e(start_e), ALU.mult))
                step(dve.tensor_reduce(starts[:, c, :], t0, AX, ALU.add))
            step(dve.tensor_copy(ranks_i[:], ranks[:]))
            step(dve.tensor_scalar(tiles_i[:], ranks_i[:], 7, None, ALU.arith_shift_right))
            step(dve.tensor_scalar(lanes_i[:], ranks_i[:], P - 1, None, ALU.bitwise_and))
            step(dve.tensor_copy(lanes[:], lanes_i[:]))
            step(dve.tensor_copy(tiles[:], tiles_i[:]))
            step(dve.tensor_tensor(tiles[:], tiles[:], starts[:], ALU.add))
            step(dve.scalar_tensor_tensor(out=slot_of[:], in0=tiles[:], scalar=float(P), in1=lanes[:], op0=ALU.mult, op1=ALU.add))
            dve.wait_ge(ctx_ready, 8 * B)
            CT = TOP_K * TT
            step(dve.tensor_tensor(lane_hot, lanes[:].rearrange("p c t -> p (c t)").unsqueeze(2).to_broadcast((P, CT, P)),
                                   lane_ids[:].unsqueeze(1).to_broadcast((P, CT, P)), ALU.is_equal))
            step(dve.tensor_tensor(tile_hot, tiles[:].rearrange("p c t -> p (c t)").unsqueeze(2).to_broadcast((P, CT, ST1)),
                                   lane_ids[:, 0:ST1].unsqueeze(1).to_broadcast((P, CT, ST1)), ALU.is_equal))
            for c in range(TOP_K):
                ins = dve.tensor_tensor(tile_hot[:, c * TT:(c + 1) * TT, :], tile_hot[:, c * TT:(c + 1) * TT, :],
                                        token_ids[:].unsqueeze(2).to_broadcast((P, TT, ST1)), ALU.mult)
                if c < TOP_K - 1:
                    step(ins)
            ins.then_inc(onehots, 1)
            e7 = E - 1
            le = small_plan[0:1, 0:E * ST1].rearrange("p (t e) -> p t e", e=E)
            ends_1 = end_e[0:1, :].unsqueeze(1).to_broadcast((1, ST1, E))
            tile_no = lane_ids[0:1, 0:ST1]
            step(dve.tensor_tensor(le, ends_1, tile_no.unsqueeze(2).to_broadcast((1, ST1, E)), ALU.is_le))
            step(dve.tensor_reduce(plan_f[:, 0, :], le[:, :, 0:e7], AX, ALU.add))
            step(dve.scalar_tensor_tensor(out=le, in0=le, scalar=99.0, in1=ends_1, op0=ALU.mult, op1=ALU.add))
            step(dve.tensor_reduce(plan_f[:, 1, :], le, AX, ALU.min))
            step(dve.tensor_tensor(le, ends_1, plan_f[:, 1, :].unsqueeze(2).to_broadcast((1, ST1, E)), ALU.is_le))
            step(dve.tensor_reduce(plan_f[:, 2, :], le[:, :, 0:e7], AX, ALU.add))
            step(dve.tensor_copy(nxt[:], plan_f[:, 2, :]))
            step(dve.tensor_copy(plan[:, 0, :], plan_f[:, 0, :]))
            step(dve.memset(plan_f[:, 3, 0:1], 1.0))
            step(dve.tensor_tensor(plan_f[:, 3, 1:ST1], plan_f[:, 0, 1:ST1], plan_f[:, 0, 0:ST1 - 1], ALU.not_equal))
            step(dve.tensor_copy(plan[:, 1, :], plan_f[:, 3, :]))
            step(dve.tensor_tensor(plan_f[:, 4, :], plan_f[:, 2, :], plan_f[:, 0, :], ALU.not_equal))
            step(dve.tensor_tensor(plan[:, 2, :], plan_f[:, 4, :], plan_f[:, 3, :], ALU.mult))
            dve.wait_ge(gate_exp, 2)
            step(dve.tensor_scalar(r1, gate_out[:], 1.0, None, ALU.add))
            step(dve.reciprocal(gates[:, 0, :], r1))
            step(dve.tensor_tensor(gates[:, 1, :], gates[:, 0, :], gate_out[:], ALU.mult))
            dve.wait_ge(token_sum, 1)
            dve.tensor_copy(token_of[:], bank[2][:, 0:ST1]).then_inc(plan_ready, 1)

            def win_lo(c, t, flag=None):
                def op():
                    return dve.tensor_tensor(win[:, LO, c, :], raw_in[:, c, :], win[:, HI, c, :], ALU.subtract)
                if flag is None:
                    dve.wait_ge(win_hi[c], t + 1)
                    op().then_inc(win_ready[c], 1)
                    return
                with dve.If(flag != 0):
                    dve.wait_ge(win_hi[c], t + 1)
                    op().then_inc(win_ready[c], 1)
                with dve.Else():
                    dve.wait_ge(win_hi[c], t + 1)
                    dve.wait_ge(win_ready[c], t)
                    dve.tensor_copy(sink_dve[:, c:c + 1], ones[:, 0:1]).then_inc(win_ready[c], 1)

            def x_lo(t):
                dve.wait_ge(xT_hi, t + 1)
                dve.tensor_tensor(rowsT[0][:, LO, :, :].rearrange("p k q -> p (k q)"), b_xT[:],
                                  rowsT[0][:, HI, :, :].rearrange("p k q -> p (k q)"), ALU.subtract).then_inc(xT_ready, 1)

            def product(t, c):
                dve.wait_ge(silu_done, 4 * t + c + 1)
                dve.wait_ge(gT_done, 4 * t + c + 1)
                dve.tensor_tensor(gated[c % 2], b_h[c][:, CG:CF], silus[c % 2], ALU.mult).then_inc(g_done, 1)

            def g_lo(t, c):
                dve.wait_ge(gT_hi, 4 * t + c + 1)
                dve.tensor_tensor(gT[c % 2][:, LO, :, :].rearrange("p k q -> p (k q)"), b_gT[c % 2][:, 0:CG],
                                  gT[c % 2][:, HI, :, :].rearrange("p k q -> p (k q)"), ALU.subtract).then_inc(gT_ready, 1)

            def y_out(t):
                dve.wait_ge(y_part, 4 * t + CHUNKS + 2)
                dve.wait_ge(y_stored, 16 * t + 16)
                dve.tensor_copy(probs[:, 0, :], b_y[:]).then_inc(y_copied, 1)

            def tile(t, last=False):
                if not last:
                    next_new = dve.snap(dve.value_load(plan[0:1, 1, bass.ds(t + 1, 1)], min_val=0, max_val=1))
                for c in (1, 2, 3):
                    product(t, c)
                    g_lo(t, c - 1)
                    if not last:
                        win_lo(c - 1, t + 1, next_new)
                if not last:
                    x_lo(t + 1)
                g_lo(t, 3)
                if not last:
                    product(t + 1, 0)
                y_out(t)
                if not last:
                    win_lo(3, t + 1, next_new)

            win_lo(0, 0)
            x_lo(0)
            for c in (1, 2, 3):
                win_lo(c, 0)
            product(0, 0)
            with dve.Fori(0, SLOT_TILES - 1) as t:
                tile(t)
            tile(SLOT_TILES - 1, last=True)

            with dve.Fori(0, TT // 4) as q:
                for s in range(4):
                    n = 4 * q + s
                    dve.wait_ge(pair_in[s], 32 * q + 32)
                    for c in range(TOP_K):
                        dve.scalar_tensor_tensor(out=at(resid, n), in0=raw_in[:, s, c * D:(c + 1) * D], scalar=gates[:, c, bass.ds(n, 1)],
                                                 in1=at(resid, n), op0=ALU.mult, op1=ALU.add).then_inc(pair_sum, 1)
                        dve.wait_ge(pair_sum, 2 * n + c + 9)


def kernel(x, ctx_2048, mask_BxS2_bk0, L0_ffn_router_weight, L0_ffn_w_in, L0_ffn_w_out, L0_ffn_bias):
    import numpy as np
    import concourse.bacc as bacc
    from concourse.bass_utils import run_bass_kernel_spmd

    B, S, D = x.shape
    E, H = L0_ffn_w_out.shape[0], L0_ffn_w_out.shape[2]
    CG = H // CHUNKS
    w_in = np.asarray(L0_ffn_w_in).reshape(E, 2, CHUNKS, CG, D // P, P).transpose(0, 2, 5, 4, 1, 3)
    w_out = np.asarray(L0_ffn_w_out).reshape(E, D, CHUNKS, CG // P, P).transpose(0, 2, 4, 3, 1)
    arrays = {
        "x": np.asarray(x).reshape(B * S, D),
        "ctx_rows": np.asarray(ctx_2048),
        "ctx_cols": np.asarray(ctx_2048).transpose(0, 2, 1),
        "mask": np.asarray(mask_BxS2_bk0).astype(np.int32),
        "router_cols": np.asarray(L0_ffn_router_weight).T,
        "w_in": w_in.reshape(E, CHUNKS, P, -1),
        "w_out": w_out.reshape(E, CHUNKS, P, -1),
        "bias": np.asarray(L0_ffn_bias).reshape(1, D),
    }
    arrays = {name: np.ascontiguousarray(a) for name, a in arrays.items()}
    nc = bacc.Bacc("TRN2", target_bir_lowering=False, num_devices=1)
    aps = [nc.dram_tensor(name, a.shape, mybir.dt.from_np(a.dtype), kind="ExternalInput").ap()
           for name, a in arrays.items()]
    out = nc.dram_tensor("out", (B * S, D), F32, kind="ExternalOutput").ap()
    xattn_moe_kernel(nc, *aps, out)
    result = run_bass_kernel_spmd(nc, [arrays], core_ids=[0])
    return result.results[0]["out"].reshape(B, S, D)
```

```python
from contextlib import ExitStack

import concourse.bass as bass
from concourse import mybir

P = 128
F32 = mybir.dt.float32
F32R = mybir.dt.float32r
F16 = mybir.dt.float16
I32 = mybir.dt.int32
ALU = mybir.AluOpType
ACT = mybir.ActivationFunctionType
AX = mybir.AxisListType.X

TOP_K = 2
HI, LO = 0, 1
PASSES = ((HI, HI), (HI, LO), (LO, HI))
CHUNKS = 4
LN_EPS = 1e-5
NEG = -1e30
LOWEST = -3.0e38


def xattn_moe_kernel(nc, x, ctx_rows, ctx_cols, mask, router_cols, w_in, w_out, bias, out):
    T, D = x.shape
    B, M, _ = ctx_rows.shape
    E = router_cols.shape[1]
    KD = D // P
    KM = M // P
    TT = T // P
    TB = TT // B
    WI = w_in.shape[3]
    WO = w_out.shape[3]
    CF = WI // KD
    CG = CF // 2
    KS = CG // P
    SLOT_TILES = (TOP_K * T - E) // P + E
    ST1 = SLOT_TILES + 1
    SCALE = float(D) ** -0.5
    assert T % P == 0 and D == 512 and M == 512 and KS == 2 and TB == 4 and WO == KS * D

    xn_dram = nc.dram_tensor("xn_rows", (T, D), F32, kind="Internal").ap()

    with ExitStack() as ctx:
        def sb(name, shape, dt=F32):
            return ctx.enter_context(nc.sbuf_tensor(name, shape, dt))

        def sem(name):
            return ctx.enter_context(nc.semaphore(name))

        def sems(name, n):
            return [sem(f"{name}{i}") for i in range(n)]

        resid = sb("resid", [P, TT, D])
        win = sb("win", [P, 2, CHUNKS, WI], F32R)
        wout = sb("wout", [P, 2, CHUNKS, WO], F32R)
        raw_in = sb("raw_in", [P, CHUNKS, WI])
        raw_out = sb("raw_out", [P, CHUNKS, WO])
        rows = sb("rows", [P, 2, D])
        rowsT = [sb(f"rowsT{i}", [P, 2, KD, P], F32R) for i in range(2)]
        work = sb("work", [P, 2, D])
        probs = sb("probs", [P, 2, D])
        gT = [sb(f"gT{i}", [P, 2, KS, P], F32R) for i in range(2)]
        ident = sb("ident", [P, P])
        ones = sb("ones", [P, P])
        earlier = sb("earlier", [P, P])
        router = sb("router", [P, KD, E])
        mvs = sb("mvs", [P, 2 * TB, 2])
        rstd = sb("rstd", [P, 2 * TB])
        shift2 = sb("shift2", [P, TB])
        bn1, bn2 = sb("bn1", [P, TB, 6]), sb("bn2", [P, TB, 6])
        ve = sb("ve", [P, 4, 2 * TB])
        smax = sb("smax", [P, TB, 6])
        valid = sb("valid", [P, B])
        gates = sb("gates", [P, TOP_K, TT])
        spare_f = sb("spare_f", [P, ST1])
        gate_of = sb("gate_of", [P, ST1])
        token_of = sb("token_of", [P, ST1], I32)
        target_of = sb("target_of", [P, ST1], I32)
        idx, idx_to = sb("idx", [P, 1], I32), sb("idx_to", [P, 1], I32)
        plan = sb("plan", [1, 4, ST1], I32)
        nxt = sb("nxt", [1, ST1], I32)
        in_use = sb("in_use", [1, 1], I32)
        sink_act, sink_dve, sink_pool = (sb(f"sink_{e}", [P, 2 * CHUNKS]) for e in ("act", "dve", "pool"))
        gate_in, gate_out = sb("gate_in", [P, TT]), sb("gate_out", [P, TT])
        slots, lanes, tiles = (sb(n, [P, TOP_K, TT]) for n in ("slots", "lanes", "tiles"))
        slots_i, lanes_i, tiles_i = (sb(n, [P, TOP_K, TT], I32) for n in ("slots_i", "lanes_i", "tiles_i"))
        lane_ids = sb("lane_ids", [P, P])
        falling = sb("falling", [P, E])
        tile_starts = sb("tile_starts", [P, TT])
        token_ids = sb("token_ids", [P, TT])
        spare_row = sb("spare_row", [P, 1])
        not_first = sb("not_first", [P, E, TT])

        win_flat = win[:].rearrange("p h c w -> p (h c w)")
        wout_flat = wout[:].rearrange("p h c w -> p (h c w)")
        CTXW = 2 * 2 * KD * M

        def ctx_part(par, kind, part, k):
            off = kind * 2 * KD * M + part * KD * M + k * M
            return win_flat[:, bass.ds(par * CTXW + off, M)]

        probsT = [wout_flat[:, i * 2 * M:(i + 1) * 2 * M].rearrange("p (h k q) -> p h k q", h=2, k=KM)
                  for i in range(2)]
        MASK_AT = 4 * M
        mask_neg = wout_flat[:, MASK_AT:MASK_AT + 2 * M]
        ones_r = wout_flat[:, MASK_AT + 2 * M:MASK_AT + 2 * M + P]
        silus = [work[:, 0, i * CG:(i + 1) * CG] for i in range(2)]
        gated = [work[:, 1, i * CG:(i + 1) * CG] for i in range(2)]
        hot = resid[:].rearrange("p t d -> p (t d)")
        CT = TOP_K * TT
        lane_hot = hot[:, 0:CT * P].rearrange("p (q l) -> p q l", l=P)
        tile_hot = hot[:, CT * P:CT * (P + 3 * ST1)].rearrange("p (q i l) -> p q i l", i=3, l=ST1)
        tables = work[:].rearrange("p h d -> p (h d)").rearrange("p (i e t) -> p i e t", e=E, t=TT)
        (logits_et, both_et, before_et, upto_et, top1_et, top2_et, eq_et, _) = (tables[:, i, :, :] for i in range(8))
        small = rows[:, 1, 0:P]
        small_plan = rows[:, 1, P:P + E * ST1]
        plan_f = probs[0:1, 1, 0:7 * ST1].rearrange("p (i t) -> p i t", i=7)
        ctx_raw = [raw_in[:, 2, :].rearrange("p (k m) -> p k m", k=KD),
                   raw_in[:, 3, :].rearrange("p (k m) -> p k m", k=KD)]
        rows2 = raw_out[:, 0, :].rearrange("p (j d) -> p j d", j=2)
        rows2T = raw_out[:, 1, :].rearrange("p (j k q) -> p j k q", j=2, k=KD)
        mask_i = raw_out[:, 2, 0:M].bitcast(I32)
        bias_bc = raw_out[:, 3, M:2 * M]

        bank = [ctx.enter_context(nc.psum_tensor(f"bank{i}", [P, 512], F32)) for i in range(8)]
        b_rowsT = bank[0:2]
        b_scores = bank[2:4]
        b_probsT, b_rows2T, b_read, b_logits = bank[4:8]
        b_h = bank[0:4]
        b_gT = bank[4:6]
        b_xT, b_y = bank[6:8]

        x_in, x_rest, ctxT_in, ctxR_in, mask_in, router_in, bias_in = (sem(n) for n in (
            "x_in", "x_rest", "ctxT_in", "ctxR_in", "mask_in", "router_in", "bias_in"))
        consts = sem("consts")
        stats, rs_in, rs_sqrt, rs_step, rstd_ready = (sem(n) for n in ("stats", "rs_in", "rs_sqrt", "rs_step", "rstd_ready"))
        rows_ready, rowsT_done, rowsT_hi, rowsT_lo = (sem(n) for n in ("rows_ready", "rowsT_done", "rowsT_hi", "rowsT_lo"))
        ctx_hi, ctx_ready = sems("ctx_hi", 2), sems("ctx_ready", 2)
        mask_done = sem("mask_done")
        scores_done, maxed, negmax, exp_done = (sem(n) for n in ("scores_done", "maxed", "negmax", "exp_done"))
        probsT_done, probsT_hi, probsT_lo, read_done = (sem(n) for n in ("probsT_done", "probsT_hi", "probsT_lo", "read_done"))
        norm_step, resid_done, mv2_done = sem("norm_step"), sem("resid_done"), sem("mv2_done")
        xn_stored = sems("xn_stored", 2)
        rows2_ready, rows2T_done, rows2T_copied, logits_done, biased, out_based = (
            sem(n) for n in ("rows2_ready", "rows2T_done", "rows2T_copied", "logits_done", "biased", "out_based"))
        route, gate_exp, chosen, counts_done, onehots, token_sum, tokens_ready, plan_ready = (
            sem(n) for n in ("route", "gate_exp", "chosen", "counts_done", "onehots", "token_sum", "tokens_ready", "plan_ready"))
        raw_sem = sems("raw", CHUNKS)
        win_hi, win_ready, wout_hi, wout_ready = (sems(n, CHUNKS) for n in ("win_hi", "win_ready", "wout_hi", "wout_ready"))
        idx_ready, gathered, xT_done, xT_hi, xT_ready = (sem(n) for n in ("idx_ready", "gathered", "xT_done", "xT_hi", "xT_ready"))
        h_ready, silu_done, g_done, gT_done, gT_hi, gT_ready = (
            sem(n) for n in ("h_ready", "silu_done", "g_done", "gT_done", "gT_hi", "gT_ready"))
        y_part, y_copied, idx_to_ready, y_added = sem("y_part"), sem("y_copied"), sem("idx_to_ready"), sem("y_added")
        order = sem("order")

        x_tiles = x.rearrange("(n p) d -> p n d", p=P)
        out_tiles = out[0:T, :].rearrange("(n p) d -> p n d", p=P)
        xn_tiles = xn_dram.rearrange("(n p) d -> p n d", p=P)

        def at(tensor, i):
            return tensor[:, bass.ds(i, 1), :].rearrange("p o d -> p (o d)")

        def col(tensor, i):
            return tensor[:, bass.ds(i, 1)]

        block = ctx.enter_context(nc.Block())

        def ctx_pieces(b, j, last=False):
            pieces = []
            if not last:
                pieces.append((0, b + 1, j))
            if j < TB // 2:
                pieces.append((1, b, j + KM // 2))
            elif not last:
                pieces.append((1, b + 1, j - TB // 2))
            return pieces

        @block.sync
        def _(sp):
            def load_ctx(kind, b):
                src = (ctx_cols, ctx_rows)[kind]
                sp.dma_start(ctx_raw[kind], src[bass.ds(b, 1), :, :].rearrange("o (k p) m -> p (o k) m", p=P)).then_inc(
                    (ctxT_in, ctxR_in)[kind], 16)

            def load_mask(b):
                sp.dma_start(mask_i, mask[bass.ds(b, 1), :].to_broadcast((P, M))).then_inc(mask_in, 16)

            def load_win(c, e, **kw):
                sp.dma_start(raw_in[:, c, :], w_in[bass.ds(e, 1), c, :, :].rearrange("o p w -> (o p) w"), **kw).then_inc(raw_sem[c], 16)

            def load_wout(c, e, **kw):
                sp.dma_start(raw_out[:, c, :], w_out[bass.ds(e, 1), c, :, :].rearrange("o p w -> (o p) w"), **kw).then_inc(raw_sem[c], 16)

            def store_batch(b):
                for j in range(TB):
                    n = TB * b + j
                    sp.wait_ge(rows2_ready, n + 1)
                    sp.sem_inc(order, 1)
                    sp.dma_start(at(xn_tiles, n), rows2[:, j % 2, :]).then_inc(xn_stored[j % 2], 16)
                sp.wait_ge(biased, TB * b + TB)
                sp.sem_inc(order, 1)
                sp.dma_start(out_tiles[:, bass.ds(TB * b, TB), :], resid[:, bass.ds(TB * b, TB), :]).then_inc(out_based, 16)

            for p in range(2):
                sp.sem_inc(xn_stored[p], 16)
            sp.dma_start(resid[:, 0:TB, :], x_tiles[:, 0:TB, :]).then_inc(x_in, 16)
            load_ctx(0, 0)
            load_mask(0)
            load_ctx(1, 0)
            sp.dma_start(resid[:, TB:TT, :], x_tiles[:, TB:TT, :]).then_inc(x_rest, 16)
            sp.dma_start(router[:], router_cols.rearrange("(k p) e -> p k e", p=P)).then_inc(router_in, 16)
            sp.dma_start(bias_bc, bias.to_broadcast((P, D))).then_inc(bias_in, 16)
            for c in (0, 1):
                load_win(c, 0)

            def batch(b, first=False, last=False):
                if not last:
                    sp.wait_ge(ctx_ready[0], KD * b + KD)
                    sp.sem_inc(order, 1)
                    load_ctx(0, b + 1)
                    sp.wait_ge(mask_done, 2 * b + 2)
                    sp.sem_inc(order, 1)
                    load_mask(b + 1)
                    sp.wait_ge(ctx_ready[1], KM * b + KM)
                    sp.sem_inc(order, 1)
                    load_ctx(1, b + 1)
                if not first:
                    store_batch(b - 1)

            batch(0, first=True)
            with sp.Fori(1, B - 1) as b:
                batch(b)
            batch(B - 1, last=True)
            sp.wait_ge(ctx_ready[0], KD * B)
            sp.wait_ge(ctx_ready[1], KM * B)
            load_win(2, 0)
            load_win(3, 0)
            store_batch(B - 1)
            sp.wait_ge(biased, TT)
            sp.wait_ge(logits_done, TT + 2)
            for p in range(2):
                sp.wait_ge(xn_stored[p], 16 * (TT // 2) + 16)
            sp.wait_ge(mask_done, 2 * B)
            for c in range(CHUNKS):
                sp.wait_ge(raw_sem[c], 16)
                load_wout(c, 0)
            sp.wait_ge(plan_ready, 1)
            first = sp.snap(sp.value_load(plan[0:1, 0, 0:1], min_val=0, max_val=E - 1))
            for c in range(CHUNKS):
                sp.wait_ge(win_ready[c], 1)
                sp.wait_ge(wout_ready[c], 1)
                sp.sem_inc(order, 1)
                load_win(c, first, cond=(first != 0))
                load_wout(c, first, cond=(first != 0))
            with sp.Fori(0, SLOT_TILES) as t:
                live = sp.snap(sp.value_load(plan[0:1, 3, bass.ds(t, 1)], min_val=0, max_val=1))
                with sp.If(live != 0):
                    wanted = sp.snap(sp.value_load(plan[0:1, 2, bass.ds(t, 1)], min_val=0, max_val=1))
                    e = sp.snap(sp.value_load(nxt[0:1, bass.ds(t, 1)], min_val=0, max_val=E - 1))
                    split = sp.snap(t + 2)
                    for c in range(CHUNKS):
                        sp.wait_ge(wout_ready[c], split)
                        sp.sem_inc(order, 1)
                        sp.wait_ge(h_ready, 4 * t + c + 1)
                        sp.sem_inc(order, 1)
                        load_win(c, e, cond=(wanted != 0))
                        load_wout(c, e, cond=(wanted != 0))
            used = sp.snap(sp.value_load(in_use[0:1, 0:1], min_val=1, max_val=SLOT_TILES))
            loads = sp.snap(32 * used + 64)
            sp.wait_ge(y_added, 16 * used + 16)
            sp.sem_inc(order, 1)
            for c in range(CHUNKS):
                sp.wait_ge(raw_sem[c], loads)
                sp.sem_inc(order, 1)

        @block.gpsimd
        def _(pool):
            pool.memset(ones[:], 1.0).then_inc(consts, 1)
            pool.memset(work[:, 0, :], 0.0).then_inc(consts, 1)
            pool.memset(mask_neg.bitcast(F32), 0.0).then_inc(consts, 1)
            pool.memset(ones_r.bitcast(F32), 1.0).then_inc(consts, 1)
            pool.memset(not_first[:], 1.0).then_inc(consts, 1)
            pool.wait_ge(consts, 5)
            pool.dma_start(out[T:T + P, :], work[:, 0, :]).then_inc(y_added, 16)
            pool.affine_select(ident[:], ones[:], pattern=[[-1, P]], compare_op=ALU.is_equal, fill=0.0,
                               base=0, channel_multiplier=1).then_inc(consts, 1)
            pool.affine_select(earlier[:], ones[:], pattern=[[1, P]], compare_op=ALU.is_gt, fill=0.0,
                               base=0, channel_multiplier=-1).then_inc(consts, 1)
            pool.memset(not_first[:, :, 0:1], 0.0).then_inc(consts, 1)
            for dst, pattern, base, per_partition in (
                    (lane_ids, [[1, P]], 0, 0), (falling, [[-1, E]], E, 0), (tile_starts, [[P, TT]], 0, 0),
                    (token_ids, [[P, TT]], 1, 1), (spare_row, [[0, 1]], T + 1, 1)):
                pool.iota(dst[:], pattern=pattern, base=base, channel_multiplier=per_partition,
                          allow_small_or_imprecise_dtypes=True).then_inc(consts, 1)

            def ctx_lo(kind, b, k):
                pool.wait_ge(ctx_hi[kind], KD * b + k + 1)
                pool.sem_inc(order, 1)
                pool.tensor_tensor(ctx_part(b % 2, kind, LO, k), ctx_raw[kind][:, k, :],
                                   ctx_part(b % 2, kind, HI, k), ALU.subtract).then_inc(ctx_ready[kind], 1)

            def add_bias(b, j):
                n = TB * b + j
                pool.wait_ge(rows2_ready, n + 1)
                pool.sem_inc(order, 1)
                pool.tensor_tensor(at(resid, n), at(resid, n), bias_bc, ALU.add).then_inc(biased, 1)

            def batch(b, first=False, last=False):
                for j in range(TB):
                    for piece in ctx_pieces(b, j, last):
                        ctx_lo(*piece)
                if not first:
                    for j in range(TB):
                        add_bias(b - 1, j)

            for k in range(KD):
                ctx_lo(0, 0, k)
            for k in range(KM // 2):
                ctx_lo(1, 0, k)
            pool.wait_ge(bias_in, 16)
            batch(0, first=True)
            with pool.Fori(1, B - 1) as b:
                batch(b)
            batch(B - 1, last=True)
            for j in range(TB):
                add_bias(B - 1, j)

            def lo_of(kind, c):
                dst, raw = ((win, raw_in), (wout, raw_out))[kind]
                return pool.tensor_tensor(dst[:, LO, c, :], raw[:, c, :], dst[:, HI, c, :], ALU.subtract)

            def wout_lo(c, r, flag):
                with pool.If(flag != 0):
                    pool.wait_ge(wout_hi[c], r + 1)
                    lo_of(1, c).then_inc(wout_ready[c], 1)
                with pool.Else():
                    pool.wait_ge(wout_hi[c], r + 1)
                    pool.wait_ge(wout_ready[c], r)
                    pool.sem_inc(order, 1)
                    pool.tensor_copy(sink_pool[:, c:c + 1], ones[:, 0:1]).then_inc(wout_ready[c], 1)

            def gather(t):
                pool.wait_ge(idx_ready, t + 1)
                pool.sem_inc(order, 1)
                pool.indirect_dma_start(rows[:, 0, :], None, xn_dram,
                                        bass.IndirectOffsetOnAxis(idx[:], 0)).then_inc(gathered, 16)

            for c in range(CHUNKS):
                pool.wait_ge(win_hi[c], 1)
                lo_of(0, c).then_inc(win_ready[c], 1)
            for c in range(CHUNKS):
                pool.wait_ge(wout_hi[c], 1)
                lo_of(1, c).then_inc(wout_ready[c], 1)
            for p in range(2):
                pool.wait_ge(xn_stored[p], 16 * (TT // 2) + 16)
            pool.wait_ge(out_based, 16 * B)
            pool.wait_ge(y_added, 16)
            pool.wait_ge(tokens_ready, 1)
            pool.tensor_copy(idx[:], token_of[:, 0:1]).then_inc(idx_ready, 1)
            gather(0)
            pool.wait_ge(plan_ready, 1)
            changed = pool.snap(pool.value_load(plan[0:1, 1, 0:1], min_val=0, max_val=1))
            for c in range(CHUNKS - 1):
                wout_lo(c, 1, changed)

            def tile(t):
                this_changed = pool.snap(pool.value_load(plan[0:1, 1, bass.ds(t, 1)], min_val=0, max_val=1))
                next_changed = pool.snap(pool.value_load(plan[0:1, 1, bass.ds(t + 1, 1)], min_val=0, max_val=1))
                pool.wait_ge(gathered, 16 * t + 16)
                pool.tensor_copy(idx[:], col(token_of, t + 1)).then_inc(idx_ready, 1)
                pool.wait_ge(xT_done, t + 1)
                gather(t + 1)
                wout_lo(CHUNKS - 1, t + 1, this_changed)
                for c in range(CHUNKS - 1):
                    wout_lo(c, t + 2, next_changed)
                pool.wait_ge(y_added, 16 * t + 16)
                pool.tensor_copy(idx_to[:], col(target_of, t)).then_inc(idx_to_ready, 1)
                pool.wait_ge(idx_to_ready, t + 1)
                pool.wait_ge(y_copied, t + 2)
                pool.sem_inc(order, 1)
                pool.indirect_dma_start(out, bass.IndirectOffsetOnAxis(idx_to[:], 0), probs[:, 0, :], None,
                                        compute_op=ALU.add).then_inc(y_added, 16)

            with pool.Fori(0, SLOT_TILES) as t:
                live = pool.snap(pool.value_load(plan[0:1, 3, bass.ds(t, 1)], min_val=0, max_val=1))
                with pool.If(live != 0):
                    tile(t)
            used = pool.snap(pool.value_load(in_use[0:1, 0:1], min_val=1, max_val=SLOT_TILES))
            pool.wait_ge(gathered, 16 * used + 16)

        @block.tensor
        def _(pe):
            pe.sem_inc(rowsT_done, 2)
            pe.sem_inc(scores_done, 2)
            pe.sem_inc(probsT_done, 2)
            pe.sem_inc(read_done, 2)
            pe.sem_inc(rows2T_done, 2)
            pe.sem_inc(logits_done, 2)
            pe.sem_inc(gT_done, 2)
            pe.sem_inc(y_part, 2)
            pe.wait_ge(consts, 7)

            def transposes(dst, src, n):
                for k in range(n):
                    mm = pe.transpose(dst[:, k * P:(k + 1) * P], src[:, k * P:(k + 1) * P], ident[:])
                return mm

            def rows_turn(n, j):
                pe.wait_ge(rows_ready, n + 1)
                pe.wait_ge(rowsT_lo, n + 1)
                transposes(b_rowsT[j % 2], rows[:, j % 2, :], KD).then_inc(rowsT_done, 1)

            def scores(n, b, j):
                par = b % 2
                pe.wait_ge(ctx_ready[0], KD * b + KD)
                pe.wait_ge(mask_done, 2 * b + 2)
                pe.wait_ge(rowsT_lo, n + 3)
                pe.wait_ge(exp_done, n + 1)
                pe.matmul(b_scores[j % 2][:], ones_r, mask_neg[:, bass.ds(par * M, M)], start=True, stop=False)
                m = 0
                for k in range(KD):
                    for s, v in PASSES:
                        m += 1
                        mm = pe.matmul(b_scores[j % 2][:], rowsT[j % 2][:, s, k, :], ctx_part(par, 0, v, k),
                                       start=False, stop=(m == 3 * KD))
                mm.then_inc(scores_done, 1)

            def probs_turn(n, j):
                pe.wait_ge(exp_done, n + 3)
                pe.wait_ge(probsT_lo, n + 1)
                transposes(b_probsT, probs[:, j % 2, :], KM).then_inc(probsT_done, 1)

            def read(n, b, j):
                par = b % 2
                pe.wait_ge(ctx_ready[1], KM * b + KM)
                pe.wait_ge(probsT_lo, n + 2)
                pe.wait_ge(resid_done, n + 2)
                m = 0
                for k in range(KM):
                    for s, v in PASSES:
                        mm = pe.matmul(b_read[:], probsT[j % 2][:, s, k, :], ctx_part(par, 1, v, k),
                                       start=(m == 0), stop=(m == 3 * KM - 1))
                        m += 1
                mm.then_inc(read_done, 1)

            def rows2_turn(b, j):
                n = TB * b + j
                pe.wait_ge(rows2_ready, n + 1)
                pe.wait_ge(rows2T_copied, n + 1)
                transposes(b_rows2T, rows2[:, j % 2, :], KD).then_inc(rows2T_done, 1)

            def logits(b, j):
                n = TB * b + j
                pe.wait_ge(rows2T_copied, n + 2)
                for k in range(KD):
                    mm = pe.matmul(b_logits[:, bass.ds(n * E, E)], rows2T[:, j % 2, k, :], router[:, k, :],
                                   start=(k == 0), stop=(k == KD - 1))
                mm.then_inc(logits_done, 1)

            def slot(b, j, first=False, last=False):
                n = TB * b + j
                if not (last and j == TB - 1):
                    rows_turn(n + 1, j + 1)
                scores(n, b, j)
                if not first and j == 2:
                    rows2_turn(b - 1, 0)
                if not first and j == 3:
                    logits(b - 1, 1)
                    rows2_turn(b - 1, 2)
                if not (first and j == 0):
                    probs_turn(n - 1, j - 1)
                if not (first and j < 2):
                    read(n - 2, b - 1 if j < 2 else b, j - 2)
                if not first and j == 2:
                    logits(b - 1, 0)
                    rows2_turn(b - 1, 1)
                if not first and j == 3:
                    logits(b - 1, 2)
                    rows2_turn(b - 1, 3)
                    logits(b - 1, 3)

            pe.wait_ge(router_in, 16)
            rows_turn(0, 0)
            for j in range(TB):
                slot(0, j, first=True)
            with pe.Fori(1, B - 1) as b:
                for j in range(TB):
                    slot(b, j)
            for j in range(TB):
                slot(B - 1, j, last=True)
            probs_turn(TT - 1, TB - 1)
            read(TT - 2, B - 1, TB - 2)
            read(TT - 1, B - 1, TB - 1)
            for j in range(TB):
                rows2_turn(B - 1, j)
                logits(B - 1, j)

            pe.wait_ge(chosen, 1)
            pe.matmul(bank[0][:, 0:TT * E], earlier[:], both_et, start=True, stop=False)
            pe.matmul(bank[0][:, 0:TT * E], ones[:], before_et, start=False, stop=True)
            pe.matmul(bank[1][:, 0:E], ones[:], upto_et[:, :, TT - 1], start=True, stop=True).then_inc(counts_done, 1)
            pe.wait_ge(onehots, 4)
            for q in range(CT):
                mm = pe.matmul(bank[2][:, 0:2 * ST1], lane_hot[:, q, :], tile_hot[:, q, 1:3, :].rearrange("p i l -> p (i l)"),
                               start=(q == 0), stop=(q == CT - 1))
            mm.then_inc(token_sum, 1)

            def x_turn(t):
                pe.wait_ge(gathered, 16 * t + 16)
                pe.wait_ge(xT_ready, t + 1)
                transposes(b_xT, rows[:, 0, :], KD).then_inc(xT_done, 1)

            def up(t, c):
                if c == 0:
                    pe.wait_ge(xT_ready, t + 2)
                pe.wait_ge(win_ready[c], t + 2)
                pe.wait_ge(g_done, 4 * t + c + 1)
                m = 0
                for k in range(KD):
                    for s, v in PASSES:
                        mm = pe.matmul(b_h[c][:], rowsT[0][:, s, k, :], win[:, v, c, k * CF:(k + 1) * CF],
                                       start=(m == 0), stop=(m == 3 * KD - 1))
                        m += 1
                mm.then_inc(h_ready, 1)

            def g_turn(t, c):
                pe.wait_ge(g_done, 4 * t + c + 5)
                pe.wait_ge(gT_ready, 4 * t + c + 1)
                transposes(b_gT[c % 2], gated[c % 2], KS).then_inc(gT_done, 1)

            def down(t, c):
                pe.wait_ge(gT_ready, 4 * t + c + 3)
                pe.wait_ge(wout_ready[c], t + 2)
                if c == 0:
                    pe.wait_ge(y_copied, t + 1)
                m = 0
                for k in range(KS):
                    for s, v in PASSES:
                        mm = pe.matmul(b_y[:], gT[c % 2][:, s, k, :], wout[:, v, c, k * D:(k + 1) * D],
                                       start=(c == 0 and m == 0), stop=(c == CHUNKS - 1 and m == 3 * KS - 1))
                        m += 1
                mm.then_inc(y_part, 1)

            def tile(t):
                up(t, 1)
                g_turn(t, 0)
                up(t, 2)
                g_turn(t, 1)
                down(t, 0)
                up(t, 3)
                g_turn(t, 2)
                down(t, 1)
                x_turn(t + 1)
                down(t, 2)
                g_turn(t, 3)
                up(t + 1, 0)
                down(t, 3)

            x_turn(0)
            up(0, 0)
            pe.wait_ge(plan_ready, 1)
            with pe.Fori(0, SLOT_TILES) as t:
                live = pe.snap(pe.value_load(plan[0:1, 3, bass.ds(t, 1)], min_val=0, max_val=1))
                with pe.If(live != 0):
                    tile(t)

        @block.scalar
        def _(act):
            act.sem_inc(exp_done, 2)
            act.sem_inc(rows2T_copied, 1)

            def root(r, cols):
                act.wait_ge(rs_in, r + 1)
                act.activation(ve[:, 1, cols], ve[:, 0, cols], ACT.Sqrt).then_inc(rs_sqrt, 1)

            def ctx_hi_of(kind, b, k):
                act.wait_ge((ctxT_in, ctxR_in)[kind], 16 * b + 16)
                act.activation(ctx_part(b % 2, kind, HI, k), ctx_raw[kind][:, k, :], ACT.Copy).then_inc(ctx_hi[kind], 1)

            def split_ctx(b, j, first, last):
                for kind, of, k in ctx_pieces(b, j, last):
                    if kind == 0:
                        act.wait_ge(scores_done, TB * b + 2)
                    elif j >= 2:
                        act.wait_ge(read_done, TB * b + 2)
                    elif not first:
                        act.wait_ge(read_done, TB * b - TB + 2)
                    ctx_hi_of(kind, of, k)

            def rows_hi(n, j):
                act.wait_ge(rowsT_done, n + 3)
                act.wait_ge(scores_done, n + 1)
                act.activation(rowsT[j % 2][:, HI, :, :].rearrange("p k q -> p (k q)"), b_rowsT[j % 2][:], ACT.Copy).then_inc(rowsT_hi, 1)

            def exps(n, j):
                act.wait_ge(negmax, n + 1)
                act.wait_ge(probsT_done, n + 1)
                act.activation(probs[:, j % 2, :], b_scores[j % 2][:], ACT.Exp, bias=smax[:, j, 1:2], scale=SCALE,
                               accum_out=smax[:, j, 2:3]).then_inc(exp_done, 1)

            def probs_hi(n, j):
                act.wait_ge(probsT_done, n + 3)
                act.wait_ge(read_done, n + 1)
                act.activation(probsT[j % 2][:, HI, :, :].rearrange("p k q -> p (k q)"), b_probsT[:], ACT.Copy).then_inc(probsT_hi, 1)

            def normalise2(b, j):
                n = TB * b + j
                act.wait_ge(rstd_ready, 2 * b + 6)
                act.wait_ge(rows2T_done, n + 1)
                act.wait_ge(xn_stored[j % 2], 32 * b + 16 * (j // 2) + 16)
                act.activation(rows2[:, j % 2, :], at(resid, n), ACT.Identity, bias=shift2[:, j:j + 1],
                               scale=rstd[:, j:j + 1]).then_inc(rows2_ready, 1)

            def rows2_copy(b, j):
                n = TB * b + j
                act.wait_ge(rows2T_done, n + 3)
                act.wait_ge(logits_done, n + 1)
                act.activation(rows2T[:, j % 2, :, :].rearrange("p k q -> p (k q)"), b_rows2T[:], ACT.Copy).then_inc(rows2T_copied, 1)

            def slot(b, j, first=False, last=False):
                n = TB * b + j
                if not (last and j == TB - 1):
                    rows_hi(n + 1, j + 1)
                if j == 2:
                    root(b + 1, slice(TB, 2 * TB) if first else slice(0, TB) if last else slice(0, 2 * TB))
                if not first and j == 2:
                    normalise2(b - 1, 0)
                    normalise2(b - 1, 1)
                if not first and j == 3:
                    rows2_copy(b - 1, 1)
                    normalise2(b - 1, 2)
                if not (first and j == 0):
                    probs_hi(n - 1, j - 1)
                exps(n, j)
                split_ctx(b, j, first, last)
                if not first and j == 2:
                    rows2_copy(b - 1, 0)
                if not first and j == 3:
                    rows2_copy(b - 1, 2)
                    normalise2(b - 1, 3)
                    rows2_copy(b - 1, 3)

            root(0, slice(TB, 2 * TB))
            for k in range(KD):
                ctx_hi_of(0, 0, k)
            for k in range(KM // 2):
                ctx_hi_of(1, 0, k)
            rows_hi(0, 0)
            for j in range(TB):
                slot(0, j, first=True)
            with act.Fori(1, B - 1) as b:
                for j in range(TB):
                    slot(b, j)
            for j in range(TB):
                slot(B - 1, j, last=True)
            probs_hi(TT - 1, TB - 1)
            root(B + 1, slice(0, TB))
            normalise2(B - 1, 0)
            normalise2(B - 1, 1)
            for j in range(TB):
                rows2_copy(B - 1, j)
                if j + 2 < TB:
                    normalise2(B - 1, j + 2)

            act.wait_ge(gate_exp, 1)
            act.activation(gate_out[:], gate_in[:], ACT.Exp).then_inc(gate_exp, 1)

            def hi_of(kind, c):
                dst, raw = ((win, raw_in), (wout, raw_out))[kind]
                return act.activation(dst[:, HI, c, :], raw[:, c, :], ACT.Copy)

            def split(kind, c, r, flag, used=None):
                done = (win_hi, wout_hi)[kind][c]
                with act.If(flag != 0):
                    if used is not None:
                        act.wait_ge(*used)
                    act.wait_ge(raw_sem[c], 32 * r + 32)
                    hi_of(kind, c).then_inc(done, 1)
                with act.Else():
                    act.wait_ge(done, r)
                    act.copy(sink_act[:, kind * CHUNKS + c:kind * CHUNKS + c + 1], ones[:, 0:1]).then_inc(done, 1)

            def win_split(c, t, flag):
                split(0, c, t + 1, flag, (h_ready, 4 * t + c - 3))

            def wout_split(c, t, flag):
                split(1, c, t + 1, flag, (y_part, 4 * t + c - 1))

            def x_hi(t):
                act.wait_ge(xT_done, t + 1)
                act.activation(rowsT[0][:, HI, :, :].rearrange("p k q -> p (k q)"), b_xT[:], ACT.Copy).then_inc(xT_hi, 1)

            def silu(t, c):
                act.wait_ge(h_ready, 4 * t + c + 1)
                act.wait_ge(g_done, 4 * t + c + 3)
                act.activation(silus[c % 2], b_h[c][:, 0:CG], ACT.Silu).then_inc(silu_done, 1)

            def g_hi(t, c):
                act.wait_ge(gT_done, 4 * t + c + 3)
                act.wait_ge(y_part, 4 * t + c + 1)
                act.activation(gT[c % 2][:, HI, :, :].rearrange("p k q -> p (k q)"), b_gT[c % 2][:, 0:CG], ACT.Copy).then_inc(gT_hi, 1)

            def tile(t):
                silu(t, 1)
                g_hi(t, 0)
                next_changed = act.snap(act.value_load(plan[0:1, 1, bass.ds(t + 1, 1)], min_val=0, max_val=1))
                win_split(0, t + 1, next_changed)
                silu(t, 2)
                g_hi(t, 1)
                win_split(1, t + 1, next_changed)
                this_changed = act.snap(act.value_load(plan[0:1, 1, bass.ds(t, 1)], min_val=0, max_val=1))
                wout_split(CHUNKS - 1, t, this_changed)
                silu(t, 3)
                g_hi(t, 2)
                win_split(2, t + 1, next_changed)
                act.wait_ge(h_ready, 4 * t + 4)
                x_hi(t + 1)
                wout_split(0, t + 1, next_changed)
                g_hi(t, 3)
                silu(t + 1, 0)
                win_split(3, t + 1, next_changed)
                wout_split(1, t + 1, next_changed)
                wout_split(2, t + 1, next_changed)

            for c in range(CHUNKS):
                act.wait_ge(raw_sem[c], 16)
                hi_of(0, c).then_inc(win_hi[c], 1)
            for c in range(CHUNKS):
                act.wait_ge(raw_sem[c], 32)
                hi_of(1, c).then_inc(wout_hi[c], 1)
            act.wait_ge(plan_ready, 1)
            changed = act.snap(act.value_load(plan[0:1, 1, 0:1], min_val=0, max_val=1))
            split(0, 0, 1, changed)
            x_hi(0)
            for c in (1, 2, 3):
                split(0, c, 1, changed)
            silu(0, 0)
            for c in range(CHUNKS - 1):
                split(1, c, 1, changed)
            with act.Fori(0, SLOT_TILES) as t:
                live = act.snap(act.value_load(plan[0:1, 3, bass.ds(t, 1)], min_val=0, max_val=1))
                with act.If(live != 0):
                    tile(t)

        @block.vector
        def _(dve):
            dve.sem_inc(rowsT_lo, 2)
            dve.sem_inc(probsT_lo, 1)
            dve.sem_inc(resid_done, 2)
            dve.sem_inc(g_done, 4)
            dve.sem_inc(gT_ready, 2)
            dve.sem_inc(xT_ready, 1)
            dve.sem_inc(y_copied, 1)

            FIRST, SECOND, BOTH = slice(TB, 2 * TB), slice(0, TB), slice(0, 2 * TB)

            def stats1(b, js):
                for j in js:
                    n = TB * b + j
                    dve.bn_stats(bn1[:, j, :], at(resid, n)).then_inc(stats, 1)
                dve.wait_ge(stats, 2 * TB * b + 2 * js[0] + 2)
                if not (isinstance(b, int) and b == 0):
                    dve.wait_ge(rows_ready, TB * b - TB + js[-1] + 1)
                dve.sem_inc(order, 1)
                for j in js:
                    dve.bn_aggr(mvs[:, TB + j, :], bn1[:, j, :]).then_inc(stats, 1)

            def root_in(r, cols):
                dve.tensor_scalar(ve[:, 0, cols], mvs[:, cols, 1], LN_EPS, None, ALU.add).then_inc(rs_in, 1)

            def root_out(r, cols, second):
                n = cols
                dve.wait_ge(rs_sqrt, r + 1)
                dve.reciprocal(ve[:, 2, n], ve[:, 1, n]).then_inc(rs_step, 1)
                dve.wait_ge(rs_step, 4 * r + 1)
                dve.tensor_tensor(ve[:, 3, n], ve[:, 2, n], ve[:, 2, n], ALU.mult).then_inc(rs_step, 1)
                dve.wait_ge(rs_step, 4 * r + 2)
                dve.tensor_tensor(ve[:, 3, n], ve[:, 3, n], ve[:, 0, n], ALU.mult).then_inc(rs_step, 1)
                dve.wait_ge(rs_step, 4 * r + 3)
                dve.tensor_scalar(ve[:, 3, n], ve[:, 3, n], -0.5, 1.5, ALU.mult, ALU.add).then_inc(rs_step, 1)
                dve.wait_ge(rs_step, 4 * r + 4)
                dve.tensor_tensor(rstd[:, n], ve[:, 2, n], ve[:, 3, n], ALU.mult).then_inc(rstd_ready, 1)
                dve.wait_ge(rstd_ready, 2 * r + 1)
                if second:
                    dve.scalar_tensor_tensor(out=shift2[:], in0=mvs[:, 0:TB, 0], scalar=-1.0, in1=rstd[:, 0:TB],
                                             op0=ALU.mult, op1=ALU.mult).then_inc(rstd_ready, 1)
                    dve.wait_ge(rstd_ready, 2 * r + 2)
                else:
                    dve.sem_inc(rstd_ready, 1)

            def normalise(n, j):
                dve.wait_ge(rowsT_done, n + 1)
                dve.tensor_scalar(rows[:, j % 2, :], at(resid, n), mvs[:, TB + j, 0:1],
                                  rstd[:, TB + j:TB + j + 1], ALU.subtract, ALU.mult).then_inc(rows_ready, 1)

            def rows_lo(n, j):
                dve.wait_ge(rowsT_hi, n + 1)
                hl = rowsT[j % 2]
                dve.tensor_tensor(hl[:, LO, :, :].rearrange("p k q -> p (k q)"), b_rowsT[j % 2][:],
                                  hl[:, HI, :, :].rearrange("p k q -> p (k q)"), ALU.subtract).then_inc(rowsT_lo, 1)

            def mask_row(b):
                dve.wait_ge(mask_in, 16 * b + 16)
                dve.tensor_scalar(mask_neg[0:1, bass.ds((b % 2) * M, M)], mask_i[0:1, :], -1.0, -NEG / SCALE,
                                  ALU.add, ALU.mult).then_inc(mask_done, 1)
                dve.tensor_reduce(valid[:, bass.ds(b, 1)], mask_i, AX, ALU.max).then_inc(mask_done, 1)

            def row_max(n, j):
                dve.wait_ge(scores_done, n + 3)
                dve.tensor_reduce(smax[:, j, 0:1], b_scores[j % 2][:], AX, ALU.max).then_inc(maxed, 1)
                dve.wait_ge(maxed, n + 1)
                dve.tensor_scalar(smax[:, j, 1:2], smax[:, j, 0:1], -SCALE, None, ALU.mult).then_inc(negmax, 1)

            def probs_lo(n, j):
                dve.wait_ge(probsT_hi, n + 1)
                dve.tensor_tensor(probsT[j % 2][:, LO, :, :].rearrange("p k q -> p (k q)"), b_probsT[:],
                                  probsT[j % 2][:, HI, :, :].rearrange("p k q -> p (k q)"), ALU.subtract).then_inc(probsT_lo, 1)

            def residual(n, b, j):
                dve.wait_ge(exp_done, n + 3)
                dve.reciprocal(smax[:, j, 3:4], smax[:, j, 2:3]).then_inc(norm_step, 1)
                dve.wait_ge(norm_step, 3 * n + 1)
                dve.tensor_tensor(smax[:, j, 4:5], smax[:, j, 3:4], valid[:, bass.ds(b, 1)], ALU.mult).then_inc(norm_step, 1)
                dve.wait_ge(norm_step, 3 * n + 2)
                dve.wait_ge(read_done, n + 3)
                dve.scalar_tensor_tensor(out=at(resid, n), in0=b_read[:], scalar=smax[:, j, 4:5], in1=at(resid, n),
                                         op0=ALU.mult, op1=ALU.add).then_inc(resid_done, 1)
                dve.wait_ge(resid_done, n + 3)
                dve.sem_inc(order, 1)
                dve.bn_stats(bn2[:, j, :], at(resid, n)).then_inc(norm_step, 1)
                dve.wait_ge(norm_step, 3 * n + 3)
                dve.sem_inc(order, 1)
                dve.bn_aggr(mvs[:, j, :], bn2[:, j, :]).then_inc(mv2_done, 1)

            def slot(b, j, first=False, last=False):
                n = TB * b + j
                if not (last and j == TB - 1):
                    rows_lo(n + 1, j + 1)
                if j == 2:
                    root_out(b + 1, FIRST if first else SECOND if last else BOTH, not first)
                if not (last and j >= 2):
                    normalise(n + 2, (j + 2) % TB)
                row_max(n, j)
                if not (first and j == 0):
                    probs_lo(n - 1, (j - 1) % TB)
                if not (first and j < 2):
                    residual(n - 2, b - 1 if j < 2 else b, (j - 2) % TB)
                if not last and j < 2:
                    if j == 0:
                        dve.wait_ge(x_rest, 16)
                        dve.sem_inc(order, 1)
                    stats1(b + 1, (2 * j, 2 * j + 1))
                if j == 1:
                    if not last:
                        dve.wait_ge(stats, 2 * TB * b + 4 * TB)
                    if not first:
                        dve.wait_ge(mv2_done, TB * b)
                    root_in(b + 1, FIRST if first else SECOND if last else BOTH)
                if j == 3 and not last:
                    mask_row(b + 1)

            dve.wait_ge(consts, 3)
            dve.wait_ge(x_in, 16)
            stats1(0, (0, 1))
            stats1(0, (2, 3))
            dve.wait_ge(stats, 2 * TB)
            root_in(0, FIRST)
            mask_row(0)
            root_out(0, FIRST, False)
            normalise(0, 0)
            normalise(1, 1)
            rows_lo(0, 0)
            for j in range(TB):
                slot(0, j, first=True)
            with dve.Fori(1, B - 1) as b:
                for j in range(TB):
                    slot(b, j)
            for j in range(TB):
                slot(B - 1, j, last=True)
            probs_lo(TT - 1, TB - 1)
            residual(TT - 2, B - 1, TB - 2)
            residual(TT - 1, B - 1, TB - 1)
            dve.wait_ge(mv2_done, TT)
            root_in(B + 1, SECOND)
            root_out(B + 1, SECOND, True)

            steps = [0]

            def step(ins):
                ins.then_inc(route, 1)
                steps[0] += 1
                dve.wait_ge(route, steps[0])

            def by_expert(table):
                return table.rearrange("p e t -> p t e")

            def per_tile(a):
                return a.unsqueeze(1).to_broadcast((P, E, TT))

            def per_expert(a):
                return a.unsqueeze(2).to_broadcast((P, E, TT))

            def flat(a):
                return a.rearrange("p e t -> p (e t)")

            max1, max2, first1, first2, gate_sum = (small[:, i * TT:(i + 1) * TT] for i in range(5))
            n_tiles, ends, starts = (small[:, 5 * TT + i * E:5 * TT + (i + 1) * E] for i in range(3))
            dve.wait_ge(logits_done, TT + 2)
            dve.wait_ge(consts, 13)
            dve.wait_ge(y_added, 16)
            step(dve.tensor_copy(by_expert(logits_et), b_logits[:, 0:TT * E].rearrange("p (t e) -> p t e", e=E)))

            def pick(top, first, most):
                step(dve.tensor_reduce(most, by_expert(logits_et), AX, ALU.max))
                step(dve.tensor_tensor(eq_et, logits_et, per_tile(most), ALU.is_equal))
                step(dve.tensor_tensor(eq_et, eq_et, per_expert(falling[:]), ALU.mult))
                step(dve.tensor_reduce(first, by_expert(eq_et), AX, ALU.max))
                step(dve.tensor_tensor(top, per_expert(falling[:]), per_tile(first), ALU.is_equal))

            pick(top1_et, first1, max1)
            step(dve.tensor_scalar(eq_et, top1_et, 2.0, -1.0, ALU.mult, ALU.add))
            step(dve.scalar_tensor_tensor(out=logits_et, in0=eq_et, scalar=LOWEST, in1=logits_et, op0=ALU.mult, op1=ALU.min))
            pick(top2_et, first2, max2)
            step(dve.tensor_tensor(both_et, top1_et, top2_et, ALU.add))
            step(dve.tensor_tensor_scan(flat(upto_et), flat(not_first[:]), flat(both_et), 0.0, ALU.mult, ALU.add))
            dve.tensor_tensor(before_et, upto_et, both_et, ALU.subtract).then_inc(chosen, 1)
            dve.tensor_tensor(gate_in[:], max2, max1, ALU.subtract).then_inc(gate_exp, 1)
            dve.wait_ge(gate_exp, 2)
            step(dve.tensor_scalar(gate_sum, gate_out[:], 1.0, None, ALU.add))
            step(dve.reciprocal(gates[:, 0, :], gate_sum))
            step(dve.tensor_tensor(gates[:, 1, :], gates[:, 0, :], gate_out[:], ALU.mult))
            dve.wait_ge(counts_done, 1)
            step(dve.tensor_tensor(eq_et, per_expert(bank[1][:, 0:E]), per_tile(tile_starts[:]), ALU.is_gt))
            step(dve.tensor_reduce(n_tiles, eq_et, AX, ALU.add))
            step(dve.tensor_tensor_scan(ends, ones[:, 0:E], n_tiles, 0.0, ALU.mult, ALU.add))
            step(dve.tensor_tensor(starts, ends, n_tiles, ALU.subtract))
            step(dve.scalar_tensor_tensor(out=logits_et, in0=per_expert(starts), scalar=float(P),
                                          in1=bank[0][:, 0:TT * E].rearrange("p (e t) -> p e t", e=E),
                                          op0=ALU.mult, op1=ALU.add))
            for c, top in enumerate((top1_et, top2_et)):
                step(dve.tensor_tensor(eq_et, top, logits_et, ALU.mult))
                step(dve.tensor_reduce(slots[:, c, :], by_expert(eq_et), AX, ALU.add))
            step(dve.tensor_copy(slots_i[:], slots[:]))
            step(dve.tensor_scalar(tiles_i[:], slots_i[:], 7, None, ALU.arith_shift_right))
            step(dve.tensor_scalar(lanes_i[:], slots_i[:], P - 1, None, ALU.bitwise_and))
            step(dve.tensor_copy(lanes[:], lanes_i[:]))
            step(dve.tensor_copy(tiles[:], tiles_i[:]))
            dve.wait_ge(out_based, 16 * B)

            def per_choice(a, n):
                return a.rearrange("p c t -> p (c t)").unsqueeze(2).to_broadcast((P, CT, n))

            dve.tensor_tensor(lane_hot, per_choice(lanes[:], P),
                              lane_ids[:].unsqueeze(1).to_broadcast((P, CT, P)), ALU.is_equal).then_inc(onehots, 1)
            step(dve.tensor_tensor(tile_hot[:, :, 0, :], per_choice(tiles[:], ST1),
                                   lane_ids[:, 0:ST1].unsqueeze(1).to_broadcast((P, CT, ST1)), ALU.is_equal))
            for c in range(TOP_K):
                dve.tensor_tensor(tile_hot[:, c * TT:(c + 1) * TT, 1, :], tile_hot[:, c * TT:(c + 1) * TT, 0, :],
                                  token_ids[:].unsqueeze(2).to_broadcast((P, TT, ST1)), ALU.mult).then_inc(onehots, 1)
            dve.tensor_tensor(tile_hot[:, :, 2, :], tile_hot[:, :, 0, :], per_choice(gates[:], ST1), ALU.mult).then_inc(onehots, 1)
            ends_1 = ends[0:1, :].unsqueeze(1).to_broadcast((1, ST1, E))
            le = small_plan[0:1, :].rearrange("p (t e) -> p t e", e=E)
            tile_no = lane_ids[0:1, 0:ST1]
            expert, run_end, expert_next, run_start, other = (plan_f[:, i, :] for i in range(5))
            step(dve.tensor_tensor(le, ends_1, tile_no.unsqueeze(2).to_broadcast((1, ST1, E)), ALU.is_le))
            step(dve.tensor_reduce(expert, le[:, :, 0:E - 1], AX, ALU.add))
            step(dve.scalar_tensor_tensor(out=le, in0=le, scalar=float(P), in1=ends_1, op0=ALU.mult, op1=ALU.add))
            step(dve.tensor_reduce(run_end, le, AX, ALU.min))

            dve.wait_ge(token_sum, 1)
            slot_tokens = bank[2][:, 0:ST1]
            dve.tensor_scalar(token_of[:], slot_tokens, -1.0, 0.0, ALU.add, ALU.max).then_inc(tokens_ready, 1)
            step(dve.tensor_scalar(spare_f[:], slot_tokens, 0.0, spare_row[:, 0:1], ALU.is_equal, ALU.mult))
            step(dve.scalar_tensor_tensor(out=target_of[:], in0=slot_tokens, scalar=-1.0, in1=spare_f[:], op0=ALU.add, op1=ALU.add))
            step(dve.tensor_copy(gate_of[:], bank[2][:, ST1:2 * ST1]))

            step(dve.tensor_tensor(le, ends_1, run_end.unsqueeze(2).to_broadcast((1, ST1, E)), ALU.is_le))
            step(dve.tensor_reduce(expert_next, le[:, :, 0:E - 1], AX, ALU.add))
            step(dve.tensor_copy(nxt[:], expert_next))
            step(dve.tensor_copy(plan[:, 0, :], expert))
            step(dve.memset(run_start[:, 0:1], 1.0))
            step(dve.tensor_tensor(run_start[:, 1:ST1], expert[:, 1:ST1], expert[:, 0:ST1 - 1], ALU.not_equal))
            step(dve.tensor_copy(plan[:, 1, 1:ST1], run_start[:, 1:ST1]))
            step(dve.tensor_scalar(plan[:, 1, 0:1], expert[:, 0:1], 0.0, None, ALU.not_equal))
            step(dve.tensor_tensor(other, expert_next, expert, ALU.not_equal))
            step(dve.tensor_tensor(plan[:, 2, :], other, run_start, ALU.mult))
            step(dve.tensor_tensor(plan[:, 3, :], tile_no, ends[0:1, E - 1:E].to_broadcast((1, ST1)), ALU.is_lt))
            dve.tensor_copy(in_use[:], ends[0:1, E - 1:E]).then_inc(plan_ready, 1)

            def win_lo(c, r, flag):
                with dve.If(flag != 0):
                    dve.wait_ge(win_hi[c], r + 1)
                    dve.tensor_tensor(win[:, LO, c, :], raw_in[:, c, :], win[:, HI, c, :], ALU.subtract).then_inc(win_ready[c], 1)
                with dve.Else():
                    dve.wait_ge(win_hi[c], r + 1)
                    dve.wait_ge(win_ready[c], r)
                    dve.tensor_copy(sink_dve[:, c:c + 1], ones[:, 0:1]).then_inc(win_ready[c], 1)

            def x_lo(t):
                dve.wait_ge(xT_hi, t + 1)
                dve.tensor_tensor(rowsT[0][:, LO, :, :].rearrange("p k q -> p (k q)"), b_xT[:],
                                  rowsT[0][:, HI, :, :].rearrange("p k q -> p (k q)"), ALU.subtract).then_inc(xT_ready, 1)

            def product(t, c):
                dve.wait_ge(silu_done, 4 * t + c + 1)
                dve.wait_ge(gT_done, 4 * t + c + 1)
                dve.tensor_tensor(gated[c % 2], b_h[c][:, CG:CF], silus[c % 2], ALU.mult).then_inc(g_done, 1)

            def g_lo(t, c):
                dve.wait_ge(gT_hi, 4 * t + c + 1)
                dve.tensor_tensor(gT[c % 2][:, LO, :, :].rearrange("p k q -> p (k q)"), b_gT[c % 2][:, 0:CG],
                                  gT[c % 2][:, HI, :, :].rearrange("p k q -> p (k q)"), ALU.subtract).then_inc(gT_ready, 1)

            def y_out(t):
                dve.wait_ge(y_part, 4 * t + CHUNKS + 2)
                dve.wait_ge(y_added, 16 * t + 16)
                dve.sem_inc(order, 1)
                dve.tensor_scalar(probs[:, 0, :], b_y[:], col(gate_of, t), None, ALU.mult).then_inc(y_copied, 1)

            def tile(t):
                next_changed = dve.snap(dve.value_load(plan[0:1, 1, bass.ds(t + 1, 1)], min_val=0, max_val=1))
                for c in (1, 2, 3):
                    product(t, c)
                    g_lo(t, c - 1)
                    win_lo(c - 1, t + 2, next_changed)
                x_lo(t + 1)
                g_lo(t, 3)
                product(t + 1, 0)
                y_out(t)
                win_lo(3, t + 2, next_changed)

            dve.wait_ge(plan_ready, 1)
            changed = dve.snap(dve.value_load(plan[0:1, 1, 0:1], min_val=0, max_val=1))
            win_lo(0, 1, changed)
            x_lo(0)
            for c in (1, 2, 3):
                win_lo(c, 1, changed)
            product(0, 0)
            with dve.Fori(0, SLOT_TILES) as t:
                live = dve.snap(dve.value_load(plan[0:1, 3, bass.ds(t, 1)], min_val=0, max_val=1))
                with dve.If(live != 0):
                    tile(t)


def kernel(x, ctx_2048, mask_BxS2_bk0, L0_ffn_router_weight, L0_ffn_w_in, L0_ffn_w_out, L0_ffn_bias):
    import numpy as np
    import concourse.bacc as bacc
    from concourse.bass_utils import run_bass_kernel_spmd

    B, S, D = x.shape
    E, H = L0_ffn_w_out.shape[0], L0_ffn_w_out.shape[2]
    CG = H // CHUNKS
    w_in = np.asarray(L0_ffn_w_in).reshape(E, 2, CHUNKS, CG, D // P, P).transpose(0, 2, 5, 4, 1, 3)
    w_out = np.asarray(L0_ffn_w_out).reshape(E, D, CHUNKS, CG // P, P).transpose(0, 2, 4, 3, 1)
    arrays = {
        "x": np.asarray(x).reshape(B * S, D),
        "ctx_rows": np.asarray(ctx_2048),
        "ctx_cols": np.asarray(ctx_2048).transpose(0, 2, 1),
        "mask": np.asarray(mask_BxS2_bk0).astype(np.int32),
        "router_cols": np.asarray(L0_ffn_router_weight).T,
        "w_in": w_in.reshape(E, CHUNKS, P, -1),
        "w_out": w_out.reshape(E, CHUNKS, P, -1),
        "bias": np.asarray(L0_ffn_bias).reshape(1, D),
    }
    arrays = {name: np.ascontiguousarray(a) for name, a in arrays.items()}
    nc = bacc.Bacc("TRN2", target_bir_lowering=False, num_devices=1)
    aps = [nc.dram_tensor(name, a.shape, mybir.dt.from_np(a.dtype), kind="ExternalInput").ap()
           for name, a in arrays.items()]
    out = nc.dram_tensor("out", (B * S + P, D), F32, kind="ExternalOutput").ap()
    xattn_moe_kernel(nc, *aps, out)
    result = run_bass_kernel_spmd(nc, [arrays], core_ids=[0])
    return result.results[0]["out"][:B * S].reshape(B, S, D)
```

```python
from contextlib import ExitStack

import concourse.bass as bass
from concourse import mybir

P = 128
F32 = mybir.dt.float32
F32R = mybir.dt.float32r
I32 = mybir.dt.int32
ALU = mybir.AluOpType
ACT = mybir.ActivationFunctionType
AX = mybir.AxisListType.X

TOP_K = 2
HI, LO = 0, 1
PASSES = ((HI, HI), (HI, LO), (LO, HI))
CHUNKS = 4
LN_EPS = 1e-5
NEG = -1e30
LOWEST = -3.0e38


def xattn_moe_kernel(nc, x, ctx_rows, ctx_cols, mask, router_cols, w_in, w_out, bias, out):
    T, D = x.shape
    B, M, _ = ctx_rows.shape
    E = router_cols.shape[1]
    KD = D // P
    KM = M // P
    TT = T // P
    TB = TT // B
    WI = w_in.shape[3]
    WO = w_out.shape[3]
    CF = WI // KD
    CG = CF // 2
    KS = CG // P
    SLOT_TILES = (TOP_K * T - E) // P + E
    SLOTS_T = SLOT_TILES + 2 + SLOT_TILES % 2
    SCALE = float(D) ** -0.5
    assert T % P == 0 and D == 512 and M == 512 and KS == 2 and TB == 4 and WO == KS * D and B % 2 == 0

    xn_dram = nc.dram_tensor("xn_rows", (T, D), F32, kind="Internal").ap()

    with ExitStack() as ctx:
        def sb(name, shape, dt=F32):
            return ctx.enter_context(nc.sbuf_tensor(name, shape, dt))

        def sem(name):
            return ctx.enter_context(nc.semaphore(name))

        def sems(name, n):
            return [sem(f"{name}{i}") for i in range(n)]

        resid = sb("resid", [P, TT, D])
        win = sb("win", [P, 2, CHUNKS, WI], F32R)
        wout = sb("wout", [P, 2, CHUNKS, WO], F32R)
        raw_in = sb("raw_in", [P, CHUNKS, WI])
        raw_out = sb("raw_out", [P, CHUNKS, WO])
        rows = sb("rows", [P, 2, D])
        rowsT = [sb(f"rowsT{i}", [P, 2, KD, P], F32R) for i in range(2)]
        work = sb("work", [P, 2, D])
        probs = sb("probs", [P, 2, D])
        gT = [sb(f"gT{i}", [P, 2, KS, P], F32R) for i in range(2)]
        ident = sb("ident", [P, P])
        ones = sb("ones", [P, P])
        not_earlier = sb("not_earlier", [P, P])
        router = sb("router", [P, KD, E])
        mvs = sb("mvs", [P, 2 * TB, 2])
        rstd = sb("rstd", [P, 2 * TB])
        shift2 = sb("shift2", [P, TB])
        bn1, bn2 = sb("bn1", [P, TB, 6]), sb("bn2", [P, TB, 6])
        ve = sb("ve", [P, 4, 2 * TB])
        smax = sb("smax", [P, TB, 6])
        valid, mask_scale = sb("valid", [P, B]), sb("mask_scale", [1, 1])
        gates = sb("gates", [P, TOP_K, TT])
        marks = sb("marks", [P, 3, TOP_K, TT], F32R)
        spare_f = sb("spare_f", [P, SLOTS_T])
        gate_of = sb("gate_of", [P, SLOTS_T])
        token_of = sb("token_of", [P, SLOTS_T], I32)
        target_of = sb("target_of", [P, SLOTS_T], I32)
        idx, idx_to = sb("idx", [P, 1], I32), sb("idx_to", [P, 1], I32)
        plan = sb("plan", [1, 4, SLOTS_T], I32)
        nxt = sb("nxt", [1, SLOTS_T], I32)
        in_use = sb("in_use", [1, 1], I32)
        sink_act, sink_dve, sink_pool = (sb(f"sink_{e}", [P, 2 * CHUNKS]) for e in ("act", "dve", "pool"))
        gate_in, gate_out = sb("gate_in", [P, TT]), sb("gate_out", [P, TT])
        slots, slots_i = sb("slots", [P, TOP_K, TT]), sb("slots_i", [P, TOP_K, TT], I32)
        places, places_i = sb("places", [P, 2, TOP_K, TT]), sb("places_i", [P, 2, TOP_K, TT], I32)
        lane_ids = sb("lane_ids", [P, P])
        falling = sb("falling", [P, E])
        tile_starts = sb("tile_starts", [P, TT])
        token_ids = sb("token_ids", [P, TT])
        spare_row = sb("spare_row", [P, 1])
        not_first = sb("not_first", [P, E, TT])

        win_flat = win[:].rearrange("p h c w -> p (h c w)")
        wout_flat = wout[:].rearrange("p h c w -> p (h c w)")
        CTXW = 2 * 2 * KD * M

        def ctx_part(par, kind, part, k):
            off = kind * 2 * KD * M + part * KD * M + k * M
            return win_flat[:, bass.ds(par * CTXW + off, M)]

        probsT = [wout_flat[:, i * 2 * M:(i + 1) * 2 * M].rearrange("p (h k q) -> p h k q", h=2, k=KM)
                  for i in range(2)]
        MASK_AT = 4 * M
        mask_neg = wout_flat[:, MASK_AT:MASK_AT + 2 * M]
        ones_r = wout_flat[:, MASK_AT + 2 * M:MASK_AT + 2 * M + P]
        silus = [work[:, 0, i * CG:(i + 1) * CG] for i in range(2)]
        gated = [work[:, 1, i * CG:(i + 1) * CG] for i in range(2)]
        hot = wout_flat
        CT = TOP_K * TT
        lane_hot = hot[:, 0:CT * P].rearrange("p (q l) -> p q l", l=P)
        tile_hot = hot[:, CT * P:CT * (P + 3 * SLOTS_T)].rearrange("p (q i l) -> p q i l", i=3, l=SLOTS_T)
        tables = work[:].rearrange("p h d -> p (h d)").rearrange("p (i e t) -> p i e t", e=E, t=TT)
        logits_et, slot_et, both_et, upto_et = (tables[:, i, :, :] for i in range(4))
        top_et = [tables[:, 4 + c, :, :] for c in range(TOP_K)]
        eq_et = tables[:, 6, :, :]
        tile_is = work[:].rearrange("p h d -> p (h d)")[:, 0:TT * SLOTS_T].rearrange("p (t l) -> p t l", l=SLOTS_T)
        small = rows[:, 1, 0:P]
        small_plan = rows[:, 1, P:P + E * SLOTS_T]
        plan_f = probs[0:1, 1, 0:5 * SLOTS_T].rearrange("p (i t) -> p i t", i=5)
        ctx_raw = [raw_in[:, 2, :].rearrange("p (k m) -> p k m", k=KD),
                   raw_in[:, 3, :].rearrange("p (k m) -> p k m", k=KD)]
        rows2 = raw_out[:, 0, :].rearrange("p (j d) -> p j d", j=2)
        rows2T = raw_out[:, 1, :].rearrange("p (j k q) -> p j k q", j=2, k=KD)
        mask_i = raw_out[:, 2, 0:M].bitcast(I32)

        def rows2_of(j, tail):
            return rows[:, j - 2, :] if tail and j >= 2 else rows2[:, j % 2, :]

        bias_bc = raw_out[:, 3, M:2 * M]

        bank = [ctx.enter_context(nc.psum_tensor(f"bank{i}", [P, 512], F32)) for i in range(8)]
        b_rowsT, b_probsT, b_read, b_logits = bank[0], bank[4], bank[6], bank[7]
        b_scores = bank[2:4]
        b_rows2T = [bank[1], bank[5]]
        b_h = bank[0:4]
        b_gT = bank[4:6]
        b_xT, b_y = bank[6:8]

        x_next, x_rest, ctxT_in, ctxR_in, mask_in, router_in, bias_in = (sem(n) for n in (
            "x_next", "x_rest", "ctxT_in", "ctxR_in", "mask_in", "router_in", "bias_in"))
        x_in = sems("x_in", 2)
        consts = sem("consts")
        stats, rs_in, rs_sqrt, rs_step, rstd_ready = (sem(n) for n in ("stats", "rs_in", "rs_sqrt", "rs_step", "rstd_ready"))
        rows_ready, rowsT_done, rowsT_hi, rowsT_lo = (sem(n) for n in ("rows_ready", "rowsT_done", "rowsT_hi", "rowsT_lo"))
        ctx_hi, ctx_ready = sems("ctx_hi", 2), sems("ctx_ready", 2)
        mask_done, mask_step = sem("mask_done"), sem("mask_step")
        scores_done, maxed, negmax, exp_done = (sem(n) for n in ("scores_done", "maxed", "negmax", "exp_done"))
        probsT_done, probsT_hi, probsT_lo, read_done = (sem(n) for n in ("probsT_done", "probsT_hi", "probsT_lo", "read_done"))
        norm_step, resid_done, mv2_done = sem("norm_step"), sem("resid_done"), sem("mv2_done")
        xn_stored = sems("xn_stored", 2)
        rows2_ready, rows2T_done, rows2T_copied, logits_done, biased, out_based = (
            sem(n) for n in ("rows2_ready", "rows2T_done", "rows2T_copied", "logits_done", "biased", "out_based"))
        tile_found, token_hot = sem("tile_found"), sem("token_hot")
        route, route_side, gate_exp, chosen, counts_done, onehots, token_sum, tokens_ready, plan_ready = (
            sem(n) for n in ("route", "route_side", "gate_exp", "chosen", "counts_done", "onehots", "token_sum", "tokens_ready", "plan_ready"))
        raw_sem = sems("raw", CHUNKS)
        win_hi, win_ready, wout_hi, wout_ready = (sems(n, CHUNKS) for n in ("win_hi", "win_ready", "wout_hi", "wout_ready"))
        idx_ready, gathered, xT_done, xT_hi, xT_ready = (sem(n) for n in ("idx_ready", "gathered", "xT_done", "xT_hi", "xT_ready"))
        h_ready, silu_done, g_done, gT_done, gT_hi, gT_ready = (
            sem(n) for n in ("h_ready", "silu_done", "g_done", "gT_done", "gT_hi", "gT_ready"))
        y_part, y_copied, idx_to_ready, y_added = sem("y_part"), sem("y_copied"), sem("idx_to_ready"), sem("y_added")
        table_loaded = sem("table_loaded")
        order = sem("order")

        x_tiles = x.rearrange("(n p) d -> p n d", p=P)
        out_tiles = out[0:T, :].rearrange("(n p) d -> p n d", p=P)
        xn_tiles = xn_dram.rearrange("(n p) d -> p n d", p=P)

        def at(tensor, i):
            return tensor[:, bass.ds(i, 1), :].rearrange("p o d -> p (o d)")

        def col(tensor, i):
            return tensor[:, bass.ds(i, 1)]

        FIRST, SECOND, BOTH, EARLY, LATE = (slice(*ends) for ends in (
            (TB, 2 * TB), (0, TB), (0, 2 * TB), (0, TB // 2), (TB // 2, TB)))

        block = ctx.enter_context(nc.Block())

        def ctx_pieces(b, j, last=False):
            if j == 0:
                return [(1, b, k) for k in range(KM // 2, KM)]
            if last:
                return []
            if j < 3:
                return [(0, b + 1, k) for k in range((j - 1) * (KD // 2), j * (KD // 2))]
            return [(1, b + 1, k) for k in range(KM // 2)]

        @block.sync
        def _(sp):
            def load_ctx(kind, b):
                src = (ctx_cols, ctx_rows)[kind]
                sp.dma_start(ctx_raw[kind], src[bass.ds(b, 1), :, :].rearrange("o (k p) m -> p (o k) m", p=P)).then_inc(
                    (ctxT_in, ctxR_in)[kind], 16)

            def load_mask(b):
                sp.dma_start(mask_i, mask[bass.ds(b, 1), :].to_broadcast((P, M))).then_inc(mask_in, 16)

            def load_win(c, e, **kw):
                sp.dma_start(raw_in[:, c, :], w_in[bass.ds(e, 1), c, :, :].rearrange("o p w -> (o p) w"), **kw).then_inc(raw_sem[c], 16)

            def load_wout(c, e, **kw):
                sp.dma_start(raw_out[:, c, :], w_out[bass.ds(e, 1), c, :, :].rearrange("o p w -> (o p) w"), **kw).then_inc(raw_sem[c], 16)

            def store_rows(b, tail=False):
                for j in range(TB):
                    n = TB * b + j
                    sp.wait_ge(rows2_ready, n + 1)
                    sp.sem_inc(order, 1)
                    sp.dma_start(at(xn_tiles, n), rows2_of(j, tail)).then_inc(xn_stored[j % 2], 16)

            for p in range(2):
                sp.sem_inc(xn_stored[p], 16)
            for i in range(2):
                half = slice(i * TB // 2, (i + 1) * TB // 2)
                sp.dma_start(resid[:, half, :], x_tiles[:, half, :]).then_inc(x_in[i], 16)
            load_ctx(0, 0)
            load_mask(0)
            load_ctx(1, 0)
            sp.dma_start(resid[:, TB:2 * TB, :], x_tiles[:, TB:2 * TB, :]).then_inc(x_next, 16)
            sp.dma_start(router[:], router_cols.rearrange("(k p) e -> p k e", p=P)).then_inc(router_in, 16)
            sp.dma_start(bias_bc, bias.to_broadcast((P, D))).then_inc(bias_in, 16)

            def batch(b, first=False, last=False):
                if not last:
                    sp.wait_ge(ctx_ready[0], KD * b + KD)
                    sp.sem_inc(order, 1)
                    load_ctx(0, b + 1)
                    sp.wait_ge(mask_done, 2 * b + 2)
                    sp.sem_inc(order, 1)
                    load_mask(b + 1)
                    sp.wait_ge(ctx_ready[1], KM * b + KM)
                    sp.sem_inc(order, 1)
                    load_ctx(1, b + 1)
                    if first:
                        sp.dma_start(resid[:, 2 * TB:TT, :], x_tiles[:, 2 * TB:TT, :]).then_inc(x_rest, 16)
                else:
                    for c in (0, 1):
                        load_win(c, 0)
                    sp.wait_ge(ctx_ready[0], KD * B)
                    load_win(2, 0)
                    sp.wait_ge(ctx_ready[1], KM * B)
                    load_win(3, 0)
                if not first:
                    store_rows(b - 1)

            batch(0, first=True)
            with sp.Fori(1, B - 1) as b:
                batch(b)
            batch(B - 1, last=True)
            store_rows(B - 1, tail=True)
            sp.wait_ge(biased, TT)
            sp.wait_ge(logits_done, TT + 2)
            for p in range(2):
                sp.wait_ge(xn_stored[p], 16 * (TT // 2) + 16)
            sp.wait_ge(mask_done, 2 * B)
            for c in range(CHUNKS):
                sp.wait_ge(raw_sem[c], 16)
                load_wout(c, 0)
            sp.wait_ge(plan_ready, 1)
            first = sp.snap(sp.value_load(plan[0:1, 0, 0:1], min_val=0, max_val=E - 1))
            for c in range(CHUNKS):
                sp.wait_ge(win_ready[c], 1)
                sp.wait_ge(wout_ready[c], 1)
                sp.sem_inc(order, 1)
                load_win(c, first, cond=(first != 0))
                load_wout(c, first, cond=(first != 0))
            with sp.Fori(0, SLOT_TILES) as t:
                live = sp.snap(sp.value_load(plan[0:1, 3, bass.ds(t, 1)], min_val=0, max_val=1))
                with sp.If(live != 0):
                    wanted = sp.snap(sp.value_load(plan[0:1, 2, bass.ds(t, 1)], min_val=0, max_val=1))
                    e = sp.snap(sp.value_load(nxt[0:1, bass.ds(t, 1)], min_val=0, max_val=E - 1))
                    split = sp.snap(t + 2)
                    for c in range(CHUNKS):
                        sp.wait_ge(wout_ready[c], split)
                        sp.sem_inc(order, 1)
                        sp.wait_ge(h_ready, 4 * t + c + 1)
                        sp.sem_inc(order, 1)
                        load_win(c, e, cond=(wanted != 0))
                        load_wout(c, e, cond=(wanted != 0))
            used = sp.snap(sp.value_load(in_use[0:1, 0:1], min_val=1, max_val=SLOT_TILES))
            loads = sp.snap(32 * used + 64)
            sp.wait_ge(y_added, 16 * used + 16)
            sp.sem_inc(order, 1)
            for c in range(CHUNKS):
                sp.wait_ge(raw_sem[c], loads)
                sp.sem_inc(order, 1)

        @block.gpsimd
        def _(pool):
            pool.memset(ones[:], 1.0).then_inc(consts, 1)
            pool.memset(work[:, 0, :], 0.0).then_inc(consts, 1)
            pool.memset(mask_neg.bitcast(F32), 0.0).then_inc(consts, 1)
            pool.memset(ones_r.bitcast(F32), 1.0).then_inc(consts, 1)
            pool.memset(not_first[:], 1.0).then_inc(consts, 1)
            pool.memset(not_earlier[:], -1.0).then_inc(consts, 1)
            pool.wait_ge(consts, 6)
            pool.dma_start(out[T:T + P, :], work[:, 0, :]).then_inc(y_added, 16)
            pool.affine_select(ident[:], ones[:], pattern=[[-1, P]], compare_op=ALU.is_equal, fill=0.0,
                               base=0, channel_multiplier=1).then_inc(consts, 1)
            pool.affine_select(not_earlier[:], not_earlier[:], pattern=[[-1, P]], compare_op=ALU.is_ge, fill=0.0,
                               base=0, channel_multiplier=1).then_inc(consts, 1)
            pool.memset(not_first[:, :, 0:1], 0.0).then_inc(consts, 1)
            for dst, pattern, base, per_partition in (
                    (lane_ids, [[1, P]], 0, 0), (falling, [[-1, E]], E, 0), (tile_starts, [[P, TT]], 0, 0),
                    (token_ids, [[P, TT]], 1, 1), (spare_row, [[0, 1]], T + 1, 1)):
                pool.iota(dst[:], pattern=pattern, base=base, channel_multiplier=per_partition,
                          allow_small_or_imprecise_dtypes=True).then_inc(consts, 1)

            def ctx_lo(kind, b, k):
                pool.wait_ge(ctx_hi[kind], KD * b + k + 1)
                pool.sem_inc(order, 1)
                pool.tensor_tensor(ctx_part(b % 2, kind, LO, k), ctx_raw[kind][:, k, :],
                                   ctx_part(b % 2, kind, HI, k), ALU.subtract).then_inc(ctx_ready[kind], 1)

            def add_bias(b, j):
                n = TB * b + j
                pool.wait_ge(rows2_ready, n + 1)
                pool.sem_inc(order, 1)
                pool.tensor_tensor(at(resid, n), at(resid, n), bias_bc, ALU.add).then_inc(biased, 1)

            def base_out(b):
                for j in range(TB):
                    add_bias(b, j)
                pool.wait_ge(biased, TB * b + TB)
                pool.sem_inc(order, 1)
                pool.dma_start(out_tiles[:, bass.ds(TB * b, TB), :], resid[:, bass.ds(TB * b, TB), :]).then_inc(out_based, 16)

            def batch(b, first=False, last=False):
                for j in range(TB):
                    for piece in ctx_pieces(b, j, last):
                        ctx_lo(*piece)
                if not first:
                    base_out(b - 1)

            for k in range(KD // 2, KD):
                ctx_lo(0, 0, k)
            for k in range(KM // 2):
                ctx_lo(1, 0, k)
            pool.wait_ge(bias_in, 16)
            batch(0, first=True)
            with pool.Fori(1, B - 1) as b:
                batch(b)
            batch(B - 1, last=True)
            base_out(B - 1)

            pool.wait_ge(read_done, TT + 2)
            for c in range(CHUNKS // 2, CHUNKS):
                pool.wait_ge(win_hi[c], 1)
                pool.tensor_tensor(win[:, LO, c, :], raw_in[:, c, :], win[:, HI, c, :], ALU.subtract).then_inc(win_ready[c], 1)

            def lo_of(c):
                return pool.tensor_tensor(wout[:, LO, c, :], raw_out[:, c, :], wout[:, HI, c, :], ALU.subtract)

            def wout_lo(c, r, flag):
                with pool.If(flag != 0):
                    pool.wait_ge(wout_hi[c], r + 1)
                    lo_of(c).then_inc(wout_ready[c], 1)
                with pool.Else():
                    pool.wait_ge(wout_hi[c], r + 1)
                    pool.wait_ge(wout_ready[c], r)
                    pool.sem_inc(order, 1)
                    pool.tensor_copy(sink_pool[:, c:c + 1], ones[:, 0:1]).then_inc(wout_ready[c], 1)

            def gather(t):
                pool.wait_ge(idx_ready, t + 1)
                pool.sem_inc(order, 1)
                pool.indirect_dma_start(rows[:, 0, :], None, xn_dram,
                                        bass.IndirectOffsetOnAxis(idx[:], 0)).then_inc(gathered, 16)

            def first_wout_lo(c):
                pool.wait_ge(wout_hi[c], 1)
                lo_of(c).then_inc(wout_ready[c], 1)

            for c in range(TOP_K):
                pool.wait_ge(tile_found, c + 1)
                pool.tensor_tensor(tile_hot[:, c * TT:(c + 1) * TT, 0, :], tile_is,
                                   marks[:, 0, c, :].unsqueeze(2).to_broadcast((P, TT, SLOTS_T)), ALU.mult).then_inc(token_hot, 1)
            for p in range(2):
                pool.wait_ge(xn_stored[p], 16 * (TT // 2) + 16)
            pool.wait_ge(out_based, 16 * B)
            pool.wait_ge(y_added, 16)
            pool.wait_ge(tokens_ready, 1)
            pool.tensor_copy(idx[:], token_of[:, 0:1]).then_inc(idx_ready, 1)
            gather(0)
            first_wout_lo(0)
            pool.wait_ge(gathered, 16)
            pool.tensor_copy(idx[:], token_of[:, 1:2]).then_inc(idx_ready, 1)
            pool.wait_ge(xT_done, 1)
            gather(1)
            first_wout_lo(1)
            pool.wait_ge(plan_ready, 1)
            changed = pool.snap(pool.value_load(plan[0:1, 1, 0:1], min_val=0, max_val=1))
            for c in range(CHUNKS - 1):
                wout_lo(c, 1, changed)

            def tile(t):
                this_changed = pool.snap(pool.value_load(plan[0:1, 1, bass.ds(t, 1)], min_val=0, max_val=1))
                next_changed = pool.snap(pool.value_load(plan[0:1, 1, bass.ds(t + 1, 1)], min_val=0, max_val=1))
                wout_lo(CHUNKS - 1, t + 1, this_changed)
                pool.wait_ge(gathered, 16 * t + 32)
                pool.tensor_copy(idx[:], col(token_of, t + 2)).then_inc(idx_ready, 1)
                pool.wait_ge(xT_done, t + 2)
                gather(t + 2)
                for c in range(CHUNKS - 1):
                    wout_lo(c, t + 2, next_changed)
                pool.wait_ge(y_added, 16 * t + 16)
                pool.tensor_copy(idx_to[:], col(target_of, t)).then_inc(idx_to_ready, 1)
                pool.wait_ge(idx_to_ready, t + 1)
                pool.wait_ge(y_copied, t + 2)
                pool.sem_inc(order, 1)
                pool.indirect_dma_start(out, bass.IndirectOffsetOnAxis(idx_to[:], 0), probs[:, 0, :], None,
                                        compute_op=ALU.add).then_inc(y_added, 16)

            with pool.Fori(0, SLOT_TILES) as t:
                live = pool.snap(pool.value_load(plan[0:1, 3, bass.ds(t, 1)], min_val=0, max_val=1))
                with pool.If(live != 0):
                    tile(t)
            used = pool.snap(pool.value_load(in_use[0:1, 0:1], min_val=1, max_val=SLOT_TILES))
            pool.wait_ge(gathered, 16 * used + 32)

        @block.tensor
        def _(pe):
            pe.sem_inc(rowsT_done, 2)
            pe.sem_inc(scores_done, 2)
            pe.sem_inc(probsT_done, 2)
            pe.sem_inc(read_done, 2)
            pe.sem_inc(rows2T_done, 2)
            pe.sem_inc(logits_done, 2)
            pe.sem_inc(gT_done, 2)
            pe.sem_inc(y_part, 2)
            pe.wait_ge(consts, 8)

            def transposes(dst, src, n):
                for k in range(n):
                    mm = pe.transpose(dst[:, k * P:(k + 1) * P], src[:, k * P:(k + 1) * P], ident[:])
                return mm

            def keep_clock(n):
                for _ in range(n):
                    pe.matmul(bank[3][:, 0:P], ones[:], ones[:], start=True, stop=True)

            def rows_turn(n, j):
                pe.wait_ge(rows_ready, n + 1)
                pe.wait_ge(rowsT_lo, n + 2)
                transposes(b_rowsT, rows[:, j % 2, :], KD).then_inc(rowsT_done, 1)

            def scores(n, b, j):
                par = b % 2
                pe.wait_ge(ctx_ready[0], KD * b + KD)
                pe.wait_ge(mask_done, 2 * b + 2)
                pe.wait_ge(rowsT_lo, n + 3)
                pe.wait_ge(exp_done, n + 1)
                pe.matmul(b_scores[j % 2][:], ones_r, mask_neg[:, bass.ds(par * M, M)], start=True, stop=False)
                m = 0
                for k in range(KD):
                    for s, v in PASSES:
                        m += 1
                        mm = pe.matmul(b_scores[j % 2][:], rowsT[j % 2][:, s, k, :], ctx_part(par, 0, v, k),
                                       start=False, stop=(m == 3 * KD))
                mm.then_inc(scores_done, 1)

            def probs_turn(n, j):
                pe.wait_ge(exp_done, n + 3)
                pe.wait_ge(probsT_lo, n + 1)
                transposes(b_probsT, probs[:, j % 2, :], KM).then_inc(probsT_done, 1)

            def read(n, b, j):
                par = b % 2
                pe.wait_ge(ctx_ready[1], KM * b + KM)
                pe.wait_ge(probsT_lo, n + 2)
                pe.wait_ge(resid_done, n + 2)
                m = 0
                for k in range(KM):
                    for s, v in PASSES:
                        mm = pe.matmul(b_read[:], probsT[j % 2][:, s, k, :], ctx_part(par, 1, v, k),
                                       start=(m == 0), stop=(m == 3 * KM - 1))
                        m += 1
                mm.then_inc(read_done, 1)

            def rows2_turn(b, j, tail=False):
                n = TB * b + j
                pe.wait_ge(rows2_ready, n + 1)
                pe.wait_ge(rows2T_copied, n + 1)
                transposes(b_rows2T[j % 2], rows2_of(j, tail), KD).then_inc(rows2T_done, 1)

            def logits(b, j):
                n = TB * b + j
                pe.wait_ge(rows2T_copied, n + 3)
                for k in range(KD):
                    mm = pe.matmul(b_logits[:, bass.ds(n * E, E)], rows2T[:, j % 2, k, :], router[:, k, :],
                                   start=(k == 0), stop=(k == KD - 1))
                mm.then_inc(logits_done, 1)

            def slot(b, j, first=False, last=False):
                n = TB * b + j
                second = not first and j == 3
                if not (last and j == TB - 1):
                    rows_turn(n + 1, j + 1)
                scores(n, b, j)
                if second:
                    rows2_turn(b - 1, 0)
                    rows2_turn(b - 1, 1)
                if not (first and j == 0):
                    probs_turn(n - 1, j - 1)
                if second:
                    logits(b - 1, 0)
                    logits(b - 1, 1)
                if not (first and j < 2):
                    read(n - 2, b - 1 if j < 2 else b, j - 2)
                if second:
                    rows2_turn(b - 1, 2)
                    rows2_turn(b - 1, 3)
                    logits(b - 1, 2)
                    logits(b - 1, 3)

            pe.wait_ge(stats, 2)
            keep_clock(10)
            rows_turn(0, 0)
            keep_clock(10)
            for j in range(TB):
                slot(0, j, first=True)
            pe.wait_ge(router_in, 16)
            with pe.Fori(1, B - 1) as b:
                for j in range(TB):
                    slot(b, j)
            for j in range(TB):
                slot(B - 1, j, last=True)
            probs_turn(TT - 1, TB - 1)
            read(TT - 2, B - 1, TB - 2)
            rows2_turn(B - 1, 0, tail=True)
            rows2_turn(B - 1, 1, tail=True)
            read(TT - 1, B - 1, TB - 1)
            logits(B - 1, 0)
            logits(B - 1, 1)
            keep_clock(8)
            rows2_turn(B - 1, 2, tail=True)
            rows2_turn(B - 1, 3, tail=True)
            logits(B - 1, 2)
            logits(B - 1, 3)

            pe.wait_ge(chosen, 1)
            pe.matmul(bank[0][:, 0:TT * E], not_earlier[:], both_et, start=True, stop=False)
            pe.matmul(bank[0][:, 0:TT * E], ones[:], upto_et, start=False, stop=True)
            pe.matmul(bank[1][:, 0:E], ones[:], upto_et[:, :, TT - 1], start=True, stop=True).then_inc(counts_done, 1)
            for q in range(CT):
                if q % TT == 0:
                    pe.wait_ge(onehots, 2 * (q // TT) + 2)
                    pe.wait_ge(token_hot, q // TT + 1)
                mm = pe.matmul(bank[2][:, 0:3 * SLOTS_T], lane_hot[:, q, :], tile_hot[:, q, :, :].rearrange("p i l -> p (i l)"),
                               start=(q == 0), stop=(q == CT - 1))
            mm.then_inc(token_sum, 1)
            keep_clock(12)

            def x_turn(t):
                pe.wait_ge(gathered, 16 * t + 16)
                pe.wait_ge(xT_ready, t + 1)
                transposes(b_xT, rows[:, 0, :], KD).then_inc(xT_done, 1)

            def up(t, c):
                if c == 0:
                    pe.wait_ge(xT_ready, t + 2)
                pe.wait_ge(win_ready[c], t + 2)
                pe.wait_ge(g_done, 4 * t + c + 1)
                m = 0
                for k in range(KD):
                    for s, v in PASSES:
                        mm = pe.matmul(b_h[c][:], rowsT[0][:, s, k, :], win[:, v, c, k * CF:(k + 1) * CF],
                                       start=(m == 0), stop=(m == 3 * KD - 1))
                        m += 1
                mm.then_inc(h_ready, 1)

            def g_turn(t, c):
                pe.wait_ge(g_done, 4 * t + c + 5)
                pe.wait_ge(gT_ready, 4 * t + c + 1)
                transposes(b_gT[c % 2], gated[c % 2], KS).then_inc(gT_done, 1)

            def down(t, c):
                pe.wait_ge(gT_ready, 4 * t + c + 3)
                pe.wait_ge(wout_ready[c], t + 2)
                if c == 0:
                    pe.wait_ge(y_copied, t + 1)
                m = 0
                for k in range(KS):
                    for s, v in PASSES:
                        mm = pe.matmul(b_y[:], gT[c % 2][:, s, k, :], wout[:, v, c, k * D:(k + 1) * D],
                                       start=(c == 0 and m == 0), stop=(c == CHUNKS - 1 and m == 3 * KS - 1))
                        m += 1
                mm.then_inc(y_part, 1)

            def tile(t):
                up(t, 1)
                g_turn(t, 0)
                up(t, 2)
                g_turn(t, 1)
                down(t, 0)
                x_turn(t + 1)
                up(t, 3)
                g_turn(t, 2)
                down(t, 1)
                down(t, 2)
                g_turn(t, 3)
                up(t + 1, 0)
                down(t, 3)

            x_turn(0)
            keep_clock(7)
            up(0, 0)
            pe.wait_ge(plan_ready, 1)
            with pe.Fori(0, SLOT_TILES) as t:
                live = pe.snap(pe.value_load(plan[0:1, 3, bass.ds(t, 1)], min_val=0, max_val=1))
                with pe.If(live != 0):
                    tile(t)

        @block.scalar
        def _(act):
            act.sem_inc(exp_done, 2)
            act.sem_inc(rows2T_copied, 2)

            def root(r, cols):
                act.wait_ge(rs_in, r + 1)
                act.activation(ve[:, 1, cols], ve[:, 0, cols], ACT.Sqrt).then_inc(rs_sqrt, 1)

            def ctx_hi_of(kind, b, k):
                act.wait_ge((ctxT_in, ctxR_in)[kind], 16 * b + 16)
                act.activation(ctx_part(b % 2, kind, HI, k), ctx_raw[kind][:, k, :], ACT.Copy).then_inc(ctx_hi[kind], 1)

            def split_ctx(b, j, first, last):
                for kind, of, k in ctx_pieces(b, j, last):
                    if kind == 0:
                        act.wait_ge(scores_done, TB * b + 2)
                    elif j >= 2:
                        act.wait_ge(read_done, TB * b + 2)
                    elif not first:
                        act.wait_ge(read_done, TB * b - TB + 2)
                    ctx_hi_of(kind, of, k)

            def rows_hi(n, j):
                act.wait_ge(rowsT_done, n + 3)
                act.wait_ge(scores_done, n + 1)
                act.activation(rowsT[j % 2][:, HI, :, :].rearrange("p k q -> p (k q)"), b_rowsT[:], ACT.Copy).then_inc(rowsT_hi, 1)

            def exps(n, j):
                act.wait_ge(negmax, n + 1)
                act.wait_ge(probsT_done, n + 1)
                act.activation(probs[:, j % 2, :], b_scores[j % 2][:], ACT.Exp, bias=smax[:, j, 1:2], scale=SCALE,
                               accum_out=smax[:, j, 2:3]).then_inc(exp_done, 1)

            def probs_hi(n, j):
                act.wait_ge(probsT_done, n + 3)
                act.wait_ge(read_done, n + 1)
                act.activation(probsT[j % 2][:, HI, :, :].rearrange("p k q -> p (k q)"), b_probsT[:], ACT.Copy).then_inc(probsT_hi, 1)

            def normalise2(b, j, tail=False):
                n = TB * b + j
                act.wait_ge(rstd_ready, 2 * b + (8 if tail and j >= 2 else 6))
                if not (tail and j >= 2):
                    act.wait_ge(rows2T_done, n + 1)
                    act.wait_ge(xn_stored[j % 2], 32 * b + 16 * (j // 2) + 16)
                act.activation(rows2_of(j, tail), at(resid, n), ACT.Identity, bias=shift2[:, j:j + 1],
                               scale=rstd[:, j:j + 1]).then_inc(rows2_ready, 1)

            def rows2_copy(b, j):
                n = TB * b + j
                act.wait_ge(rows2T_done, n + 3)
                act.wait_ge(logits_done, n + 1)
                act.activation(rows2T[:, j % 2, :, :].rearrange("p k q -> p (k q)"), b_rows2T[j % 2][:], ACT.Copy).then_inc(rows2T_copied, 1)

            def slot(b, j, first=False, last=False):
                n = TB * b + j
                second = not first and j == 3
                if not (last and j == TB - 1):
                    rows_hi(n + 1, j + 1)
                if j == 2:
                    root(b + 1, FIRST if first else SECOND if last else BOTH)
                if second:
                    rows2_copy(b - 1, 0)
                    rows2_copy(b - 1, 1)
                    normalise2(b - 1, 2)
                    normalise2(b - 1, 3)
                elif not (first and j == 0):
                    probs_hi(n - 1, j - 1)
                exps(n, j)
                if not first and j == 2:
                    normalise2(b - 1, 0)
                    normalise2(b - 1, 1)
                if second:
                    probs_hi(n - 1, j - 1)
                    rows2_copy(b - 1, 2)
                    rows2_copy(b - 1, 3)
                split_ctx(b, j, first, last)

            def hi_of(kind, c):
                dst, raw = ((win, raw_in), (wout, raw_out))[kind]
                return act.activation(dst[:, HI, c, :], raw[:, c, :], ACT.Copy)

            def first_win_hi(c):
                act.wait_ge(raw_sem[c], 16)
                hi_of(0, c).then_inc(win_hi[c], 1)

            act.wait_ge(consts, 1)
            act.activation(sink_act[:, 0:1], ones[:, 0:1], ACT.Sqrt).then_inc(table_loaded, 1)
            root(0, FIRST)
            for k in range(KD):
                ctx_hi_of(0, 0, k)
            rows_hi(0, 0)
            for k in range(KM // 2):
                ctx_hi_of(1, 0, k)
            for j in range(TB):
                slot(0, j, first=True)
            with act.Fori(1, B - 1) as b:
                for j in range(TB):
                    slot(b, j)
            for j in range(TB):
                slot(B - 1, j, last=True)
            act.wait_ge(read_done, TT - TB + 2)
            first_win_hi(0)
            root(B + 1, EARLY)
            probs_hi(TT - 1, TB - 1)
            normalise2(B - 1, 0, tail=True)
            normalise2(B - 1, 1, tail=True)
            first_win_hi(1)
            rows2_copy(B - 1, 0)
            rows2_copy(B - 1, 1)
            first_win_hi(2)
            root(B + 2, LATE)
            normalise2(B - 1, 2, tail=True)
            normalise2(B - 1, 3, tail=True)
            rows2_copy(B - 1, 2)
            rows2_copy(B - 1, 3)
            first_win_hi(3)

            act.wait_ge(gate_exp, 1)
            act.activation(gate_out[:], gate_in[:], ACT.Exp).then_inc(gate_exp, 1)

            def split(kind, c, r, flag, used=None):
                done = (win_hi, wout_hi)[kind][c]
                with act.If(flag != 0):
                    if used is not None:
                        act.wait_ge(*used)
                    act.wait_ge(raw_sem[c], 32 * r + 32)
                    hi_of(kind, c).then_inc(done, 1)
                with act.Else():
                    act.wait_ge(done, r)
                    act.copy(sink_act[:, kind * CHUNKS + c:kind * CHUNKS + c + 1], ones[:, 0:1]).then_inc(done, 1)

            def win_split(c, t, flag):
                split(0, c, t + 1, flag, (h_ready, 4 * t + c - 3))

            def wout_split(c, t, flag):
                split(1, c, t + 1, flag, (y_part, 4 * t + c - 1))

            def x_hi(t):
                act.wait_ge(xT_done, t + 1)
                act.activation(rowsT[0][:, HI, :, :].rearrange("p k q -> p (k q)"), b_xT[:], ACT.Copy).then_inc(xT_hi, 1)

            def silu(t, c):
                act.wait_ge(h_ready, 4 * t + c + 1)
                act.wait_ge(g_done, 4 * t + c + 3)
                act.activation(silus[c % 2], b_h[c][:, 0:CG], ACT.Silu).then_inc(silu_done, 1)

            def g_hi(t, c):
                act.wait_ge(gT_done, 4 * t + c + 3)
                act.wait_ge(y_part, 4 * t + c + 1)
                act.activation(gT[c % 2][:, HI, :, :].rearrange("p k q -> p (k q)"), b_gT[c % 2][:, 0:CG], ACT.Copy).then_inc(gT_hi, 1)

            def tile(t):
                silu(t, 1)
                g_hi(t, 0)
                next_changed = act.snap(act.value_load(plan[0:1, 1, bass.ds(t + 1, 1)], min_val=0, max_val=1))
                win_split(0, t + 1, next_changed)
                silu(t, 2)
                g_hi(t, 1)
                win_split(1, t + 1, next_changed)
                this_changed = act.snap(act.value_load(plan[0:1, 1, bass.ds(t, 1)], min_val=0, max_val=1))
                wout_split(CHUNKS - 1, t, this_changed)
                silu(t, 3)
                g_hi(t, 2)
                act.wait_ge(h_ready, 4 * t + 4)
                x_hi(t + 1)
                g_hi(t, 3)
                win_split(2, t + 1, next_changed)
                wout_split(0, t + 1, next_changed)
                silu(t + 1, 0)
                win_split(3, t + 1, next_changed)
                wout_split(1, t + 1, next_changed)
                wout_split(2, t + 1, next_changed)

            act.wait_ge(table_loaded, 1)
            act.wait_ge(token_sum, 1)
            for c in range(CHUNKS):
                act.wait_ge(raw_sem[c], 32)
                hi_of(1, c).then_inc(wout_hi[c], 1)
            act.wait_ge(plan_ready, 1)
            changed = act.snap(act.value_load(plan[0:1, 1, 0:1], min_val=0, max_val=1))
            split(0, 0, 1, changed)
            x_hi(0)
            for c in (1, 2, 3):
                split(0, c, 1, changed)
            silu(0, 0)
            for c in range(CHUNKS - 1):
                split(1, c, 1, changed)
            with act.Fori(0, SLOT_TILES) as t:
                live = act.snap(act.value_load(plan[0:1, 3, bass.ds(t, 1)], min_val=0, max_val=1))
                with act.If(live != 0):
                    tile(t)

        @block.vector
        def _(dve):
            dve.sem_inc(rowsT_lo, 2)
            dve.sem_inc(probsT_lo, 1)
            dve.sem_inc(resid_done, 2)
            dve.sem_inc(g_done, 4)
            dve.sem_inc(gT_ready, 2)
            dve.sem_inc(xT_ready, 1)
            dve.sem_inc(y_copied, 1)

            def stats1(b, js):
                for j in js:
                    n = TB * b + j
                    dve.bn_stats(bn1[:, j, :], at(resid, n)).then_inc(stats, 1)
                dve.wait_ge(stats, 2 * TB * b + 2 * js[0] + 2)
                if not (isinstance(b, int) and b == 0):
                    dve.wait_ge(rows_ready, TB * b - TB + js[-1] + 1)
                dve.sem_inc(order, 1)
                for j in js:
                    dve.bn_aggr(mvs[:, TB + j, :], bn1[:, j, :]).then_inc(stats, 1)

            def root_in(r, cols):
                dve.tensor_scalar(ve[:, 0, cols], mvs[:, cols, 1], LN_EPS, None, ALU.add).then_inc(rs_in, 1)

            def root_out(r, cols, second):
                dve.wait_ge(rs_sqrt, r + 1)
                dve.reciprocal(ve[:, 2, cols], ve[:, 1, cols]).then_inc(rs_step, 1)
                dve.wait_ge(rs_step, 4 * r + 1)
                dve.tensor_tensor(ve[:, 3, cols], ve[:, 2, cols], ve[:, 2, cols], ALU.mult).then_inc(rs_step, 1)
                dve.wait_ge(rs_step, 4 * r + 2)
                dve.tensor_tensor(ve[:, 3, cols], ve[:, 3, cols], ve[:, 0, cols], ALU.mult).then_inc(rs_step, 1)
                dve.wait_ge(rs_step, 4 * r + 3)
                dve.tensor_scalar(ve[:, 3, cols], ve[:, 3, cols], -0.5, 1.5, ALU.mult, ALU.add).then_inc(rs_step, 1)
                dve.wait_ge(rs_step, 4 * r + 4)
                dve.tensor_tensor(rstd[:, cols], ve[:, 2, cols], ve[:, 3, cols], ALU.mult).then_inc(rstd_ready, 1)
                dve.wait_ge(rstd_ready, 2 * r + 1)
                if second:
                    of = slice(cols.start, min(cols.stop, TB))
                    dve.scalar_tensor_tensor(out=shift2[:, of], in0=mvs[:, of, 0], scalar=-1.0, in1=rstd[:, of],
                                             op0=ALU.mult, op1=ALU.mult).then_inc(rstd_ready, 1)
                    dve.wait_ge(rstd_ready, 2 * r + 2)
                else:
                    dve.sem_inc(rstd_ready, 1)

            def normalise(n, j):
                dve.wait_ge(rowsT_done, n + 1)
                dve.tensor_scalar(rows[:, j % 2, :], at(resid, n), mvs[:, TB + j, 0:1],
                                  rstd[:, TB + j:TB + j + 1], ALU.subtract, ALU.mult).then_inc(rows_ready, 1)

            def rows_lo(n, j):
                dve.wait_ge(rowsT_hi, n + 1)
                hl = rowsT[j % 2]
                dve.tensor_tensor(hl[:, LO, :, :].rearrange("p k q -> p (k q)"), b_rowsT[:],
                                  hl[:, HI, :, :].rearrange("p k q -> p (k q)"), ALU.subtract).then_inc(rowsT_lo, 1)

            def mask_row(b):
                dve.wait_ge(mask_in, 16 * b + 16)
                dve.tensor_reduce(valid[:, bass.ds(b, 1)], mask_i, AX, ALU.max).then_inc(mask_done, 1)
                dve.wait_ge(mask_done, 2 * b + 1)
                dve.tensor_scalar(mask_scale[:], valid[0:1, bass.ds(b, 1)], -NEG / SCALE, None, ALU.mult).then_inc(mask_step, 1)
                dve.wait_ge(mask_step, b + 1)
                dve.tensor_scalar(mask_neg[0:1, bass.ds((b % 2) * M, M)], mask_i[0:1, :], -1.0, mask_scale[:, 0:1],
                                  ALU.add, ALU.mult).then_inc(mask_done, 1)

            def row_max(n, j):
                dve.wait_ge(scores_done, n + 3)
                dve.tensor_reduce(smax[:, j, 0:1], b_scores[j % 2][:], AX, ALU.max).then_inc(maxed, 1)
                dve.wait_ge(maxed, n + 1)
                dve.tensor_scalar(smax[:, j, 1:2], smax[:, j, 0:1], -SCALE, None, ALU.mult).then_inc(negmax, 1)

            def probs_lo(n, j):
                dve.wait_ge(probsT_hi, n + 1)
                dve.tensor_tensor(probsT[j % 2][:, LO, :, :].rearrange("p k q -> p (k q)"), b_probsT[:],
                                  probsT[j % 2][:, HI, :, :].rearrange("p k q -> p (k q)"), ALU.subtract).then_inc(probsT_lo, 1)

            def residual(n, b, j):
                dve.wait_ge(exp_done, n + 3)
                dve.reciprocal(smax[:, j, 3:4], smax[:, j, 2:3]).then_inc(norm_step, 1)
                dve.wait_ge(norm_step, 3 * n + 1)
                dve.tensor_tensor(smax[:, j, 4:5], smax[:, j, 3:4], valid[:, bass.ds(b, 1)], ALU.mult).then_inc(norm_step, 1)
                dve.wait_ge(norm_step, 3 * n + 2)
                dve.wait_ge(read_done, n + 3)
                dve.scalar_tensor_tensor(out=at(resid, n), in0=b_read[:], scalar=smax[:, j, 4:5], in1=at(resid, n),
                                         op0=ALU.mult, op1=ALU.add).then_inc(resid_done, 1)
                dve.wait_ge(resid_done, n + 3)
                dve.sem_inc(order, 1)
                dve.bn_stats(bn2[:, j, :], at(resid, n)).then_inc(norm_step, 1)
                dve.wait_ge(norm_step, 3 * n + 3)
                dve.sem_inc(order, 1)
                dve.bn_aggr(mvs[:, j, :], bn2[:, j, :]).then_inc(mv2_done, 1)

            def slot(b, j, first=False, last=False):
                n = TB * b + j
                if not (last and j == TB - 1):
                    rows_lo(n + 1, j + 1)
                if j == 2:
                    root_out(b + 1, FIRST if first else SECOND if last else BOTH, not first)
                if not (last and j >= 2):
                    normalise(n + 2, (j + 2) % TB)
                if not last and j == 1:
                    stats1(b + 1, (2, 3))
                if not last and j == 3:
                    mask_row(b + 1)
                row_max(n, j)
                if not (first and j == 0):
                    probs_lo(n - 1, (j - 1) % TB)
                if not (first and j < 2):
                    residual(n - 2, b - 1 if j < 2 else b, (j - 2) % TB)
                if not last and j == 0:
                    dve.wait_ge(x_next if first else x_rest, 16)
                    dve.sem_inc(order, 1)
                    stats1(b + 1, (0, 1))
                if j == 1:
                    if not last:
                        dve.wait_ge(stats, 2 * TB * b + 4 * TB)
                    if not first:
                        dve.wait_ge(mv2_done, TB * b)
                    root_in(b + 1, FIRST if first else SECOND if last else BOTH)

            dve.wait_ge(consts, 3)
            dve.wait_ge(x_in[0], 16)
            stats1(0, (0, 1))
            dve.wait_ge(x_in[1], 16)
            stats1(0, (2, 3))
            dve.wait_ge(stats, 2 * TB)
            root_in(0, FIRST)
            root_out(0, FIRST, False)
            normalise(0, 0)
            normalise(1, 1)
            mask_row(0)
            for k in range(KD // 2):
                dve.wait_ge(ctx_hi[0], k + 1)
                dve.tensor_tensor(ctx_part(0, 0, LO, k), ctx_raw[0][:, k, :], ctx_part(0, 0, HI, k), ALU.subtract).then_inc(ctx_ready[0], 1)
            rows_lo(0, 0)
            for j in range(TB):
                slot(0, j, first=True)
            with dve.Fori(1, B - 1) as b:
                for j in range(TB):
                    slot(b, j)
            for j in range(TB):
                slot(B - 1, j, last=True)
            dve.wait_ge(mv2_done, TT - 2)
            root_in(B + 1, EARLY)
            root_out(B + 1, EARLY, True)
            probs_lo(TT - 1, TB - 1)
            residual(TT - 2, B - 1, TB - 2)
            residual(TT - 1, B - 1, TB - 1)
            dve.wait_ge(mv2_done, TT)
            root_in(B + 2, LATE)
            root_out(B + 2, LATE, True)
            for c in range(CHUNKS // 2):
                dve.wait_ge(win_hi[c], 1)
                dve.tensor_tensor(win[:, LO, c, :], raw_in[:, c, :], win[:, HI, c, :], ALU.subtract).then_inc(win_ready[c], 1)

            steps = [0]

            def step(ins):
                ins.then_inc(route, 1)
                steps[0] += 1
                dve.wait_ge(route, steps[0])

            def by_expert(table):
                return table.rearrange("p e t -> p t e")

            def per_tile(a):
                return a.unsqueeze(1).to_broadcast((P, E, TT))

            def per_expert(a):
                return a.unsqueeze(2).to_broadcast((P, E, TT))

            def flat(a):
                return a.rearrange("p e t -> p (e t)")

            max1, max2, first1, first2, gate_sum = (small[:, i * TT:(i + 1) * TT] for i in range(5))
            n_tiles, ends, starts = (small[:, 5 * TT + i * E:5 * TT + (i + 1) * E] for i in range(3))
            dve.wait_ge(logits_done, TT + 2)
            dve.wait_ge(consts, 14)
            dve.wait_ge(y_added, 16)
            dve.wait_ge(xn_stored[1], 16 * (TT // 2) + 16)
            routed = b_logits[:, 0:TT * E].rearrange("p (t e) -> p e t", e=E)

            def pick(values, top, first, most):
                step(dve.tensor_reduce(most, by_expert(values), AX, ALU.max))
                step(dve.tensor_tensor(eq_et, values, per_tile(most), ALU.is_equal))
                step(dve.tensor_tensor(eq_et, eq_et, per_expert(falling[:]), ALU.mult))
                step(dve.tensor_reduce(first, by_expert(eq_et), AX, ALU.max))
                step(dve.tensor_tensor(top, per_expert(falling[:]), per_tile(first), ALU.is_equal))

            pick(routed, top_et[0], first1, max1)
            step(dve.scalar_tensor_tensor(out=logits_et, in0=top_et[0], scalar=LOWEST, in1=routed, op0=ALU.mult, op1=ALU.add))
            pick(logits_et, top_et[1], first2, max2)
            step(dve.tensor_tensor(both_et, top_et[0], top_et[1], ALU.add))
            dve.tensor_tensor_scan(flat(upto_et), flat(not_first[:]), flat(both_et), 0.0, ALU.mult, ALU.add).then_inc(chosen, 1)
            dve.tensor_tensor(gate_in[:], max2, max1, ALU.subtract).then_inc(gate_exp, 1)
            dve.wait_ge(gate_exp, 2)
            step(dve.tensor_scalar(gate_sum, gate_out[:], 1.0, None, ALU.add))
            step(dve.reciprocal(gates[:, 0, :], gate_sum))
            step(dve.tensor_tensor(gates[:, 1, :], gates[:, 0, :], gate_out[:], ALU.mult))
            step(dve.tensor_copy(marks[:, 1, :, :], gates[:]))
            step(dve.tensor_tensor(marks[:, 2, :, :], gates[:], marks[:, 1, :, :], ALU.subtract))
            step(dve.tensor_copy(marks[:, 0, :, :], token_ids[:].unsqueeze(1).to_broadcast((P, TOP_K, TT))))
            dve.wait_ge(counts_done, 1)
            step(dve.tensor_tensor(eq_et, per_expert(bank[1][:, 0:E]), per_tile(tile_starts[:]), ALU.is_gt))
            step(dve.tensor_reduce(n_tiles, eq_et, AX, ALU.add))
            step(dve.tensor_tensor_scan(ends, ones[:, 0:E], n_tiles, 0.0, ALU.mult, ALU.add))
            step(dve.tensor_tensor(starts, ends, n_tiles, ALU.subtract))
            step(dve.scalar_tensor_tensor(out=slot_et, in0=per_expert(starts), scalar=float(P),
                                          in1=bank[0][:, 0:TT * E].rearrange("p (e t) -> p e t", e=E),
                                          op0=ALU.mult, op1=ALU.add))
            step(dve.tensor_tensor(tables[:, 6:8, :, :], tables[:, 4:6, :, :],
                                   slot_et.unsqueeze(1).to_broadcast((P, TOP_K, E, TT)), ALU.mult))
            step(dve.tensor_reduce(slots[:], tables[:, 6:8, :, :].rearrange("p c e t -> p c t e"), AX, ALU.add))
            step(dve.tensor_copy(slots_i[:], slots[:]))
            dve.tensor_scalar(places_i[:, 0, :, :], slots_i[:], 7, None, ALU.arith_shift_right).then_inc(route_side, 1)
            step(dve.tensor_scalar(places_i[:, 1, :, :], slots_i[:], P - 1, None, ALU.bitwise_and))
            dve.wait_ge(route_side, 1)
            step(dve.tensor_copy(places[:], places_i[:]))
            tiles, lanes = places[:, 0, :, :], places[:, 1, :, :]
            for c in range(TOP_K):
                at_c = slice(c * TT, (c + 1) * TT)
                dve.tensor_tensor(lane_hot[:, at_c, :], lanes[:, c, :].unsqueeze(2).to_broadcast((P, TT, P)),
                                  lane_ids[:].unsqueeze(1).to_broadcast((P, TT, P)), ALU.is_equal).then_inc(onehots, 1)
                if c:
                    dve.wait_ge(onehots, 2 * c)
                    dve.wait_ge(token_hot, c)
                dve.tensor_tensor(tile_is, tiles[:, c, :].unsqueeze(2).to_broadcast((P, TT, SLOTS_T)),
                                  lane_ids[:, 0:SLOTS_T].unsqueeze(1).to_broadcast((P, TT, SLOTS_T)), ALU.is_equal).then_inc(tile_found, 1)
                dve.wait_ge(tile_found, c + 1)
                dve.tensor_tensor(tile_hot[:, at_c, 1:3, :].rearrange("p t i l -> p i t l"),
                                  tile_is.unsqueeze(1).to_broadcast((P, 2, TT, SLOTS_T)),
                                  marks[:, 1:3, c, :].unsqueeze(3).to_broadcast((P, 2, TT, SLOTS_T)), ALU.mult).then_inc(onehots, 1)
            ends_1 = ends[0:1, :].unsqueeze(1).to_broadcast((1, SLOTS_T, E))
            le = small_plan[0:1, :].rearrange("p (t e) -> p t e", e=E)
            tile_no = lane_ids[0:1, 0:SLOTS_T]
            expert, run_end, expert_next, run_start, other = (plan_f[:, i, :] for i in range(5))
            step(dve.tensor_tensor(le, ends_1, tile_no.unsqueeze(2).to_broadcast((1, SLOTS_T, E)), ALU.is_le))
            step(dve.tensor_reduce(expert, le[:, :, 0:E - 1], AX, ALU.add))
            step(dve.scalar_tensor_tensor(out=le, in0=le, scalar=float(P), in1=ends_1, op0=ALU.mult, op1=ALU.add))
            step(dve.tensor_reduce(run_end, le, AX, ALU.min))
            step(dve.tensor_tensor(le, ends_1, run_end.unsqueeze(2).to_broadcast((1, SLOTS_T, E)), ALU.is_le))
            step(dve.tensor_reduce(expert_next, le[:, :, 0:E - 1], AX, ALU.add))
            step(dve.tensor_copy(nxt[:], expert_next))

            dve.wait_ge(token_sum, 1)
            slot_tokens = bank[2][:, 0:SLOTS_T]
            dve.tensor_scalar(token_of[:], slot_tokens, -1.0, 0.0, ALU.add, ALU.max).then_inc(tokens_ready, 1)
            step(dve.tensor_scalar(spare_f[:], slot_tokens, 0.0, spare_row[:, 0:1], ALU.is_equal, ALU.mult))
            step(dve.scalar_tensor_tensor(out=target_of[:], in0=slot_tokens, scalar=-1.0, in1=spare_f[:], op0=ALU.add, op1=ALU.add))
            step(dve.tensor_copy(gate_of[:], bank[2][:, SLOTS_T:2 * SLOTS_T]))
            step(dve.tensor_tensor(gate_of[:], bank[2][:, 2 * SLOTS_T:3 * SLOTS_T], gate_of[:], ALU.add))

            step(dve.tensor_copy(plan[:, 0, :], expert))
            step(dve.memset(run_start[:, 0:1], 1.0))
            step(dve.tensor_tensor(run_start[:, 1:SLOTS_T], expert[:, 1:SLOTS_T], expert[:, 0:SLOTS_T - 1], ALU.not_equal))
            step(dve.tensor_copy(plan[:, 1, 1:SLOTS_T], run_start[:, 1:SLOTS_T]))
            step(dve.tensor_scalar(plan[:, 1, 0:1], expert[:, 0:1], 0.0, None, ALU.not_equal))
            step(dve.tensor_tensor(other, expert_next, expert, ALU.not_equal))
            step(dve.tensor_tensor(plan[:, 2, :], other, run_start, ALU.mult))
            step(dve.tensor_tensor(plan[:, 3, :], tile_no, ends[0:1, E - 1:E].to_broadcast((1, SLOTS_T)), ALU.is_lt))
            dve.tensor_copy(in_use[:], ends[0:1, E - 1:E]).then_inc(plan_ready, 1)

            def win_lo(c, r, flag):
                with dve.If(flag != 0):
                    dve.wait_ge(win_hi[c], r + 1)
                    dve.tensor_tensor(win[:, LO, c, :], raw_in[:, c, :], win[:, HI, c, :], ALU.subtract).then_inc(win_ready[c], 1)
                with dve.Else():
                    dve.wait_ge(win_hi[c], r + 1)
                    dve.wait_ge(win_ready[c], r)
                    dve.tensor_copy(sink_dve[:, c:c + 1], ones[:, 0:1]).then_inc(win_ready[c], 1)

            def x_lo(t):
                dve.wait_ge(xT_hi, t + 1)
                dve.tensor_tensor(rowsT[0][:, LO, :, :].rearrange("p k q -> p (k q)"), b_xT[:],
                                  rowsT[0][:, HI, :, :].rearrange("p k q -> p (k q)"), ALU.subtract).then_inc(xT_ready, 1)

            def product(t, c):
                dve.wait_ge(silu_done, 4 * t + c + 1)
                dve.wait_ge(gT_done, 4 * t + c + 1)
                dve.tensor_tensor(gated[c % 2], b_h[c][:, CG:CF], silus[c % 2], ALU.mult).then_inc(g_done, 1)

            def g_lo(t, c):
                dve.wait_ge(gT_hi, 4 * t + c + 1)
                dve.tensor_tensor(gT[c % 2][:, LO, :, :].rearrange("p k q -> p (k q)"), b_gT[c % 2][:, 0:CG],
                                  gT[c % 2][:, HI, :, :].rearrange("p k q -> p (k q)"), ALU.subtract).then_inc(gT_ready, 1)

            def y_out(t):
                dve.wait_ge(y_part, 4 * t + CHUNKS + 2)
                dve.wait_ge(y_added, 16 * t + 16)
                dve.sem_inc(order, 1)
                dve.tensor_scalar(probs[:, 0, :], b_y[:], col(gate_of, t), None, ALU.mult).then_inc(y_copied, 1)

            def tile(t):
                next_changed = dve.snap(dve.value_load(plan[0:1, 1, bass.ds(t + 1, 1)], min_val=0, max_val=1))
                for c in (1, 2, 3):
                    product(t, c)
                    g_lo(t, c - 1)
                    if c < 3:
                        win_lo(c - 1, t + 2, next_changed)
                x_lo(t + 1)
                g_lo(t, 3)
                win_lo(2, t + 2, next_changed)
                product(t + 1, 0)
                y_out(t)
                win_lo(3, t + 2, next_changed)

            dve.wait_ge(plan_ready, 1)
            changed = dve.snap(dve.value_load(plan[0:1, 1, 0:1], min_val=0, max_val=1))
            win_lo(0, 1, changed)
            x_lo(0)
            win_lo(1, 1, changed)
            for c in range(CHUNKS // 2, CHUNKS):
                dve.wait_ge(wout_hi[c], 1)
                dve.tensor_tensor(wout[:, LO, c, :], raw_out[:, c, :], wout[:, HI, c, :], ALU.subtract).then_inc(wout_ready[c], 1)

            for c in (2, 3):
                win_lo(c, 1, changed)
            product(0, 0)
            with dve.Fori(0, SLOT_TILES) as t:
                live = dve.snap(dve.value_load(plan[0:1, 3, bass.ds(t, 1)], min_val=0, max_val=1))
                with dve.If(live != 0):
                    tile(t)


def kernel(x, ctx_2048, mask_BxS2_bk0, L0_ffn_router_weight, L0_ffn_w_in, L0_ffn_w_out, L0_ffn_bias):
    import numpy as np
    import concourse.bacc as bacc
    from concourse.bass_utils import run_bass_kernel_spmd

    B, S, D = x.shape
    E, H = L0_ffn_w_out.shape[0], L0_ffn_w_out.shape[2]
    CG = H // CHUNKS
    w_in = np.asarray(L0_ffn_w_in).reshape(E, 2, CHUNKS, CG, D // P, P).transpose(0, 2, 5, 4, 1, 3)
    w_out = np.asarray(L0_ffn_w_out).reshape(E, D, CHUNKS, CG // P, P).transpose(0, 2, 4, 3, 1)
    arrays = {
        "x": np.asarray(x).reshape(B * S, D),
        "ctx_rows": np.asarray(ctx_2048),
        "ctx_cols": np.asarray(ctx_2048).transpose(0, 2, 1),
        "mask": np.asarray(mask_BxS2_bk0).astype(np.int32),
        "router_cols": np.asarray(L0_ffn_router_weight).T,
        "w_in": w_in.reshape(E, CHUNKS, P, -1),
        "w_out": w_out.reshape(E, CHUNKS, P, -1),
        "bias": np.asarray(L0_ffn_bias).reshape(1, D),
    }
    arrays = {name: np.ascontiguousarray(a) for name, a in arrays.items()}
    nc = bacc.Bacc("TRN2", target_bir_lowering=False, num_devices=1)
    aps = [nc.dram_tensor(name, a.shape, mybir.dt.from_np(a.dtype), kind="ExternalInput").ap()
           for name, a in arrays.items()]
    out = nc.dram_tensor("out", (B * S + P, D), F32, kind="ExternalOutput").ap()
    xattn_moe_kernel(nc, *aps, out)
    result = run_bass_kernel_spmd(nc, [arrays], core_ids=[0])
    return result.results[0]["out"][:B * S].reshape(B, S, D)
```
